# Optimizing a Trainium2 kernel written in Bass

```python
import numpy as np
import jax
import jax.numpy as jnp

def _softmax(x, axis=-1):
    return jax.nn.softmax(x, axis=axis)

def _gelu(x):
    return jax.nn.gelu(x, approximate=True)

def _silu(x):
    return jax.nn.silu(x)

def _sigmoid(x):
    return jax.nn.sigmoid(x)

def _layernorm(x, axis=-1, eps=1e-05):
    m = jnp.mean(x, axis=axis, keepdims=True)
    v = jnp.var(x, axis=axis, keepdims=True)
    return (x - m) / jnp.sqrt(v + eps)

def _scatter_add(tgt, idx, src, axis=0):
    return tgt.at[idx].add(src)

def _segment_sum(src, seg, n):
    return jax.ops.segment_sum(src, seg, n)
kernel_name = 'mk_gnn_resnorm_d1_gnn_r8_f27491'

def setup_inputs(seed: int=0):
    np.random.seed(seed)
    _w = jnp.asarray

    def _rec_inputs():
        import jax
        import jax.numpy as jnp
        _gk = jax.random.key(seed)
        x = -0.0003019 + 1 * jax.random.normal(jax.random.fold_in(_gk, 1), (6250, 512), jnp.float32)
        _s = jax.random.randint(jax.random.fold_in(_gk, 2), (50000,), 0, 6250, jnp.int32)
        _d = jax.random.randint(jax.random.fold_in(_gk, 3), (50000,), 0, 6250, jnp.int32)
        _loop = jnp.arange(6250, dtype=jnp.int32)
        src = jnp.concatenate([_s, _d, _loop])
        dst = jnp.concatenate([_d, _s, _loop])
        _o = jnp.argsort(dst, stable=True)
        src = src[_o]
        dst = dst[_o]
        return (x, src, dst)
    x, src, dst = _rec_inputs()

    def _L0_gnn_setup():
        import jax, jax.numpy as jnp
        import numpy as np
        N_NODES = 5000
        N_EDGES = 80000
        DIM_H = 512
        N_HEADS = 8
        D_HEAD = DIM_H // N_HEADS

        def _exphormer_attn(x, edge_index, Wq, Wk, Wv):
            N, D = x.shape
            H, d = (N_HEADS, D_HEAD)
            Q = (x @ Wq).reshape(N, H, d)
            K = (x @ Wk).reshape(N, H, d)
            V = (x @ Wv).reshape(N, H, d)
            src, dst = (edge_index[0], edge_index[1])
            scale = np.float32(1.0 / np.sqrt(d))
            score = jnp.einsum('ehd,ehd->eh', K[src], Q[dst]) * scale
            score = jnp.exp(jnp.clip(score, -5.0, 5.0))[..., None]
            msg = V[src] * score
            wV = jax.ops.segment_sum(msg, dst, num_segments=N)
            Z = jax.ops.segment_sum(score, dst, num_segments=N)
            return (wV / (Z + 1e-06)).reshape(N, D)
        key = jax.random.key(seed)
        ks = jax.random.split(key, 8)
        x = jax.random.normal(ks[0], (N_NODES, DIM_H), dtype=jnp.float32)
        edge_index = jax.random.randint(ks[1], (2, N_EDGES), 0, N_NODES, dtype=jnp.int32)
        virt_h = jax.random.normal(ks[2], (1, DIM_H), dtype=jnp.float32)
        virt_edge_index = jnp.zeros((2, 1), dtype=jnp.int32)
        s = 1.0 / np.sqrt(DIM_H)
        Wq = jax.random.normal(ks[3], (DIM_H, DIM_H), dtype=jnp.float32) * s
        Wk = jax.random.normal(ks[4], (DIM_H, DIM_H), dtype=jnp.float32) * s
        Wv = jax.random.normal(ks[5], (DIM_H, DIM_H), dtype=jnp.float32) * s
        bn_gamma = jnp.ones((DIM_H,), dtype=jnp.float32)
        bn_beta = jnp.zeros((DIM_H,), dtype=jnp.float32)
        return {'x': x, 'edge_index': edge_index, 'virt_h': virt_h, 'virt_edge_index': virt_edge_index, 'Wq': Wq, 'Wk': Wk, 'Wv': Wv, 'bn_gamma': bn_gamma, 'bn_beta': bn_beta}
    _L0_gnn_all = _L0_gnn_setup()
    _L0_gnn_in = {k: v for k, v in _L0_gnn_all.items() if k in ('virt_h', 'virt_edge_index', 'Wq', 'Wk', 'Wv', 'bn_gamma', 'bn_beta')}
    del _L0_gnn_all
    return {'x': x, 'src': src, 'dst': dst, 'L0_gnn_virt_h': _L0_gnn_in['virt_h'], 'L0_gnn_virt_edge_index': _L0_gnn_in['virt_edge_index'], 'L0_gnn_Wq': _L0_gnn_in['Wq'], 'L0_gnn_Wk': _L0_gnn_in['Wk'], 'L0_gnn_Wv': _L0_gnn_in['Wv'], 'L0_gnn_bn_gamma': _L0_gnn_in['bn_gamma'], 'L0_gnn_bn_beta': _L0_gnn_in['bn_beta']}

def reference(x, src, dst, L0_gnn_virt_h, L0_gnn_virt_edge_index, L0_gnn_Wq, L0_gnn_Wk, L0_gnn_Wv, L0_gnn_bn_gamma, L0_gnn_bn_beta):
    import jax
    import jax.numpy as jnp

    def _L0_gnn_ref(x, edge_index, virt_h, virt_edge_index, Wq, Wk, Wv, bn_gamma, bn_beta):
        import jax, jax.numpy as jnp
        import numpy as np
        N_NODES = 5000
        N_EDGES = 80000
        DIM_H = 512
        N_HEADS = 8
        D_HEAD = DIM_H // N_HEADS

        def _exphormer_attn(x, edge_index, Wq, Wk, Wv):
            N, D = x.shape
            H, d = (N_HEADS, D_HEAD)
            Q = (x @ Wq).reshape(N, H, d)
            K = (x @ Wk).reshape(N, H, d)
            V = (x @ Wv).reshape(N, H, d)
            src, dst = (edge_index[0], edge_index[1])
            scale = np.float32(1.0 / np.sqrt(d))
            score = jnp.einsum('ehd,ehd->eh', K[src], Q[dst]) * scale
            score = jnp.exp(jnp.clip(score, -5.0, 5.0))[..., None]
            msg = V[src] * score
            wV = jax.ops.segment_sum(msg, dst, num_segments=N)
            Z = jax.ops.segment_sum(score, dst, num_segments=N)
            return (wV / (Z + 1e-06)).reshape(N, D)
        h_attn = _exphormer_attn(x, edge_index, Wq, Wk, Wv)
        h = x + h_attn
        mean = jnp.mean(h, axis=0)
        var = jnp.mean(jnp.square(h - mean), axis=0)
        return (h - mean) * jax.lax.rsqrt(var + 1e-05) * bn_gamma + bn_beta
    edge_index = jnp.stack([src, dst])
    x = _layernorm(x + _L0_gnn_ref(x, edge_index, L0_gnn_virt_h, L0_gnn_virt_edge_index, L0_gnn_Wq, L0_gnn_Wk, L0_gnn_Wv, L0_gnn_bn_gamma, L0_gnn_bn_beta), axis=-1)
    return x

_drawn_inputs = setup_inputs


def setup_inputs(seed=0):
    import zlib

    import numpy as np

    out = dict(_drawn_inputs(seed))
    spreads = {'L0_gnn_bn_gamma': (1.0, 0.2), 'L0_gnn_bn_beta': (0.0, 0.1)}
    factors = {}
    for name, (base, spread) in spreads.items():
        noise = np.random.default_rng([zlib.crc32(name.encode()), seed]).standard_normal(out[name].shape)
        drawn = base * np.exp(spread * noise) if base else spread * noise
        out[name] = jnp.asarray(drawn.astype(out[name].dtype))
    for name, factor in factors.items():
        out[name] = (out[name] * factor).astype(out[name].dtype)
    return out
```

```python
from contextlib import ExitStack

import concourse.bass as bass
from concourse import mybir

F32 = mybir.dt.float32
BF16 = mybir.dt.bfloat16
I32 = mybir.dt.int32
U32 = mybir.dt.uint32
ALU = mybir.AluOpType
ACT = mybir.ActivationFunctionType
AX = mybir.AxisListType

P = 128
N_NODES, DIM, HEADS = 6250, 512, 8
D_HEAD = DIM // HEADS
N_EDGES = 106250
TILES = -(-N_NODES // P)
ROWS = TILES * P
BLOCKS = -(-N_EDGES // P)
BLOCKS_IN = BLOCKS + 1
STAIRS = BLOCKS + TILES - 1
PAIRS = -(-STAIRS // 2)
VISITS = 2 * PAIRS
VTILES = -(-(VISITS + 1) // P)
VCOLS = VTILES * P
RING = 6
ROUNDS = PAIRS // RING
Q_BANKS = 3
CHUNKS = DIM // P
SKIP = 65536.0
ACT_HEADS = 5
AGG = DIM + HEADS
LAST_ROWS = N_NODES - (TILES - 1) * P


def wait(eng, sem, value):
    if not (isinstance(value, int) and value <= 0):
        eng.wait_ge(sem, value)


def wait_apart(eng, sem, value):
    if not isinstance(value, int):
        value = eng.snap(eng.to_reg(value))
        eng.wait_ge(sem, 1)
    wait(eng, sem, value)


def project(nc, xT, wq, wk, wv, edges, dlast, kv_d, q_d, t_d, cnt_d, tabs):
    src_t, loc_t, t_row, cnt_row, iota_row, ident, kv = tabs
    with ExitStack() as ctx:
        def sb(name, shape, dt):
            return ctx.enter_context(nc.sbuf_tensor(name, shape, dt))

        def sem(name):
            return ctx.enter_context(nc.semaphore(name))

        w_sb = sb("w_sb", [P, 3, CHUNKS, DIM], F32)
        x_sb = [sb(f"x_sb{j}", [P, CHUNKS, P], F32) for j in range(2)]
        kv_sb = [sb(f"kv_sb{j}", [P, 2 * DIM], F32) for j in range(2)]
        q_sb = [sb(f"q_sb{j}", [P, 3, DIM], BF16) for j in range(2)]
        rest = sb("rest", [P, DIM], F32)
        kv_ps = [ctx.enter_context(nc.psum_tensor(f"kv_ps{j}", [P, 2 * DIM], F32)) for j in range(2)]
        q_ps = [ctx.enter_context(nc.psum_tensor(f"q_ps{j}", [P, DIM], F32)) for j in range(2)]
        tab_ps = ctx.enter_context(nc.psum_tensor("tab_ps", [P, 2, 512], F32))
        dl = sb("dl", [P, BLOCKS_IN], I32)
        k128 = sb("k128", [P, BLOCKS_IN], I32)
        ends = sb("ends", [P, BLOCKS_IN], F32)
        below = sb("below", [P, VCOLS], F32)
        v128i = sb("v128i", [P, VTILES], I32)
        v128 = sb("v128", [P, VTILES], F32)
        kf = sb("kf", [P, VTILES], F32)
        ki = sb("ki", [P, VTILES], I32)
        t128 = sb("t128", [P, VTILES], F32)
        ti = sb("ti", [P, VTILES], I32)
        rows = sb("rows", [P, VTILES, 2 * P], I32)
        loc = sb("loc", [P, VCOLS], F32)
        srcf = sb("srcf", [P, VCOLS], F32)
        skip = sb("skip", [P, VCOLS], F32)
        iota_i = sb("iota_i", [P, P], I32)
        col_i = sb("col_i", [P, 1], I32)
        col = sb("col", [P, 1], F32)
        t_bc = sb("t_bc", [64, VCOLS], I32)
        cnt = sb("cnt", [64, 1], F32)
        cnti = sb("cnti", [64, 1], I32)

        s_w = sem("s_w")
        s_x = [sem(f"s_x{j}") for j in range(2)]
        s_kvst = [sem(f"s_kvst{j}") for j in range(2)]
        s_qst = [sem(f"s_qst{j}") for j in range(2)]
        s_proj, s_kvc = sem("s_proj"), sem("s_kvc")
        s_qh, s_qr, s_qm, s_ql = sem("s_qh"), sem("s_qr"), sem("s_qm"), sem("s_ql")
        s_dl, s_iota, s_tab, s_rows = sem("s_dl"), sem("s_iota"), sem("s_tab"), sem("s_rows")
        s_visit, s_tr, s_trc, s_td, s_tb, s_cnt = (sem("s_visit"), sem("s_tr"), sem("s_trc"), sem("s_td"),
                                                   sem("s_tb"), sem("s_cnt"))
        cuts = [0, 8, 16, (TILES - 1) // 2]

        def tiles(eng, part, step):
            with eng.Fori(cuts[part], cuts[part + 1]) as i:
                for j in range(2):
                    step(i, j)

        with nc.Block() as block:
            @block.sync
            def _(sp):
                for n, w in enumerate((wq, wk, wv)):
                    sp.dma_start(w_sb[:, n, :, :], w.rearrange("(c p) n -> p c n", p=P)).then_inc(s_w, 16)
                for j in range(2):
                    sp.dma_start(x_sb[j][:, :, :], xT[j]).then_inc(s_x[j], 16)

                def step(i, j, more=True):
                    tile = 2 * i + j
                    if more:
                        sp.wait_ge(s_proj, tile + 1)
                        sp.dma_start(x_sb[j][:, :, :], xT[bass.ds(tile + 2, 1)].rearrange("a p c n -> (a p) c n")
                                     if not isinstance(tile, int) else xT[tile + 2]).then_inc(s_x[j], 16)
                    sp.wait_ge(s_ql, tile + 1)
                    sp.dma_start(q_d[bass.ds(tile * P, P), :],
                                 q_sb[j][:, :, :].rearrange("p a n -> p (a n)")).then_inc(s_qst[j], 16)
                with sp.Fori(0, cuts[3] - 1) as i:
                    for j in range(2):
                        step(i, j)
                step(cuts[3] - 1, 0)
                step(cuts[3] - 1, 1, False)
                step(cuts[3], 0, False)
                for j in range(2):
                    sp.wait_ge(s_qst[j], 16 * (cuts[3] + 1 - j))
                    sp.wait_ge(s_kvst[j], 16 * (cuts[3] + 1 - j))

            @block.gpsimd
            def _(pool):
                pool.dma_start(dl[:, :], dlast.broadcast_to([P, BLOCKS_IN])).then_inc(s_dl, 16)
                pool.iota(k128[:, :], pattern=[[P, BLOCKS_IN]], base=0, channel_multiplier=0)
                pool.iota(v128i[:, :], pattern=[[P * P, VTILES]], base=0, channel_multiplier=P)
                pool.iota(col_i[:, :], pattern=[[1, 1]], base=0, channel_multiplier=1)
                pool.iota(iota_i[:, :], pattern=[[1, P]], base=0, channel_multiplier=0).then_inc(s_iota, 1)
                pool.memset(kv[:, :, :, :], 0.0)
                pool.wait_ge(s_visit, 1)
                for a in range(VTILES):
                    pool.indirect_dma_start(rows[:, a, :], None, edges,
                                            bass.IndirectOffsetOnAxis(ki[:, a:a + 1], 0),
                                            bounds_check=BLOCKS_IN - 1, oob_is_err=False).then_inc(s_rows, 16)
                pool.dma_start(t_d.rearrange("(a p) -> p a", p=P), ti[:, :], allow_slow_non_contiguous=True).then_inc(s_td, 16)
                pool.wait_ge(s_td, 16)
                pool.dma_start(t_row[:, :], t_d.rearrange("(a n) -> a n", a=1)).then_inc(s_tb, 16)
                pool.dma_start(t_bc[:, :], t_d.rearrange("(a n) -> a n", a=1).broadcast_to([64, VCOLS])
                               ).then_inc(s_tb, 16)
                pool.wait_ge(s_cnt, 3)
                pool.dma_start(cnt_d.rearrange("(p a) -> p a", a=1), cnti[:, :], allow_slow_non_contiguous=True).then_inc(s_td, 16)
                pool.wait_ge(s_td, 32)
                pool.dma_start(cnt_row[:, :], cnt_d.rearrange("(a n) -> a n", a=1)).then_inc(s_tb, 16)
                pool.wait_ge(s_tb, 48)

            @block.tensor
            def _(pe):
                pe.wait_ge(s_w, 48)

                def step(i, j):
                    tile = 2 * i + j
                    pe.wait_ge(s_x[j], 16 * (i + 1))
                    wait(pe, s_kvc, tile - 1)
                    wait(pe, s_qr, tile - 1)
                    for n, out in enumerate((q_ps[j][:, :], kv_ps[j][:, 0:DIM], kv_ps[j][:, DIM:2 * DIM])):
                        for c in range(CHUNKS):
                            last = pe.matmul(out, x_sb[j][:, c, :], w_sb[:, n, c, :],
                                             start=(c == 0), stop=(c == CHUNKS - 1))
                    last.then_inc(s_proj, 1)
                for j in range(2):
                    step(0, j)
                with pe.Fori(1, cuts[1]) as i:
                    for j in range(2):
                        step(i, j)
                tiles(pe, 1, step)
                pe.wait_ge(s_visit, 3)
                for n, tab in enumerate((srcf, loc)):
                    if n:
                        pe.wait_ge(s_trc, 1)
                    for a in range(VTILES):
                        last = pe.transpose(tab_ps[:, a // 4, (a % 4) * P:(a % 4 + 1) * P],
                                            tab[:, a * P:(a + 1) * P], ident[:, :])
                    last.then_inc(s_tr, 1)
                tiles(pe, 2, step)
                step(cuts[3], 0)

            @block.scalar
            def _(act):
                def step(i, j):
                    tile = 2 * i + j
                    act.wait_ge(s_proj, tile + 1)
                    wait(act, s_kvst[j], 16 * i)
                    act.copy(kv_sb[j][:, :], kv_ps[j][:, :]).then_inc(s_kvc, 1)
                    act.wait_ge(s_kvc, tile + 1)
                    act.dma_start(kv_d[bass.ds(tile * P, P), :], kv_sb[j][:, :]).then_inc(s_kvst[j], 16)
                for j in range(2):
                    step(0, j)
                with act.Fori(1, cuts[3]) as i:
                    for j in range(2):
                        step(i, j)
                step(cuts[3], 0)

            @block.vector
            def _(dve):
                n_tab = [0]

                def tab(ins):
                    ins.then_inc(s_tab, 1)
                    n_tab[0] += 1
                    dve.wait_ge(s_tab, n_tab[0])

                dve.wait_ge(s_iota, 1)
                dve.wait_ge(s_dl, 16)
                tab(dve.tensor_copy(iota_row[:, :], iota_i[:, :]))
                tab(dve.tensor_copy(col[:, :], col_i[:, :]))
                tab(dve.tensor_scalar(ident[:, :], iota_row[:, :], col[:, 0:1], None, ALU.is_equal))
                tab(dve.tensor_copy(v128[:, :], v128i[:, :]))
                tab(dve.tensor_tensor(ends[:, :], dl[:, :], k128[:, :], ALU.add))
                for a in range(VTILES):
                    tab(dve.tensor_scalar(below[:, 0:BLOCKS], ends[:, 0:BLOCKS], v128[:, a:a + 1], None,
                                          ALU.is_lt))
                    tab(dve.tensor_reduce(kf[:, a:a + 1], below[:, 0:BLOCKS], AX.X, ALU.add))
                tab(dve.tensor_copy(ki[:, :], kf[:, :]))
                tab(dve.tensor_scalar(kf[:, :], kf[:, :], float(P), None, ALU.mult))
                tab(dve.tensor_tensor(t128[:, :], v128[:, :], kf[:, :], ALU.subtract))
                dve.tensor_scalar(ti[:, :], t128[:, :], 1.0 / P, None, ALU.mult).then_inc(s_visit, 1)

                def step(i, j):
                    tile = 2 * i + j
                    dve.wait_ge(s_proj, tile + 1)
                    wait(dve, s_qst[j], 16 * i)
                    dve.tensor_scalar(q_sb[j][:, 0, :], q_ps[j][:, :], D_HEAD ** -0.5, None,
                                      ALU.mult).then_inc(s_qh, 1)
                    dve.wait_ge(s_qh, tile + 1)
                    wait(dve, s_ql, tile)
                    dve.scalar_tensor_tensor(out=rest[:, :], in0=q_ps[j][:, :], scalar=D_HEAD ** -0.5,
                                             in1=q_sb[j][:, 0, :], op0=ALU.mult,
                                             op1=ALU.subtract).then_inc(s_qr, 1)
                    dve.wait_ge(s_qr, tile + 1)
                    dve.tensor_copy(q_sb[j][:, 1, :], rest[:, :]).then_inc(s_qm, 1)
                    dve.wait_ge(s_qm, tile + 1)
                    dve.tensor_tensor(q_sb[j][:, 2, :], rest[:, :], q_sb[j][:, 1, :],
                                      ALU.subtract).then_inc(s_ql, 1)
                for j in range(2):
                    step(0, j)
                with dve.Fori(1, cuts[1]) as i:
                    for j in range(2):
                        step(i, j)
                dve.wait_ge(s_rows, 16 * VTILES)
                for a in range(VTILES):
                    last = dve.tensor_scalar(loc[:, a * P:(a + 1) * P], rows[:, a, P:2 * P],
                                             t128[:, a:a + 1], None, ALU.subtract)
                tab(last)
                tab(dve.tensor_scalar(skip[:, :], loc[:, :], 0.0, SKIP, ALU.is_lt, ALU.mult))
                tab(dve.tensor_tensor(srcf[:, :].rearrange("p (a n) -> p a n", n=P), rows[:, :, 0:P],
                                      skip[:, :].rearrange("p (a n) -> p a n", n=P), ALU.add))
                tab(dve.tensor_scalar(skip[:, :], loc[:, :], float(P - 1), SKIP, ALU.is_gt, ALU.mult))
                dve.tensor_tensor(srcf[:, :], srcf[:, :], skip[:, :], ALU.add).then_inc(s_visit, 2)
                dve.wait_ge(s_tb, 32)
                dve.tensor_scalar(below[0:64, :], t_bc[:, :], col[0:64, 0:1], None,
                                  ALU.is_le).then_inc(s_cnt, 1)
                dve.wait_ge(s_cnt, 1)
                dve.tensor_reduce(cnt[:, :], below[0:64, :], AX.X, ALU.add).then_inc(s_cnt, 1)
                dve.wait_ge(s_cnt, 2)
                dve.tensor_copy(cnti[:, :], cnt[:, :]).then_inc(s_cnt, 1)
                tiles(dve, 1, step)
                half = tab_ps[:, :, :].rearrange("p a n -> p (a n)")[:, 0:VCOLS]
                dve.wait_ge(s_tr, 1)
                dve.tensor_copy(src_t[:, :], half).then_inc(s_trc, 1)
                dve.wait_ge(s_tr, 2)
                dve.tensor_copy(loc_t[:, :], half).then_inc(s_trc, 1)
                tiles(dve, 2, step)
                step(cuts[3], 0)


def attend(nc, kv_d, q_d, tabs, agg):
    src_t, loc_t, t_row, cnt_row, iota_row, ident, kv = tabs
    with ExitStack() as ctx:
        def sb(name, shape, dt):
            return ctx.enter_context(nc.sbuf_tensor(name, shape, dt))

        def ps(name, shape, dt):
            return ctx.enter_context(nc.psum_tensor(name, shape, dt))

        def sem(name):
            return ctx.enter_context(nc.semaphore(name))

        idx = sb("idx", [P, RING, 2], I32)
        q_tile = sb("q_tile", [P, 2, 3 * DIM], BF16)
        m_sb = sb("m_sb", [P, RING, 2, P], F32)
        mt_sb = sb("mt_sb", [P, RING, 2, P], BF16)
        raw = sb("raw", [P, RING, 2, HEADS], F32)
        score = sb("score", [P, RING, 2, HEADS], F32)
        zeros = sb("zeros", [P, DIM], BF16)
        idle = sb("idle", [P, 1], F32)
        acc = ps("acc", [P, 2, DIM], F32)
        z_acc = ps("z_acc", [P, 2, DIM], F32)
        t_ps = ps("t_ps", [P, 1, 4 * P], F32)
        q_ps = ps("q_ps", [P, Q_BANKS, DIM], F32)

        s_g = [[sem(f"s_g{s}_{u}") for u in range(2)] for s in range(RING)]
        s_init, s_idx, s_m, s_t, s_mt, s_qx = (sem("s_init"), sem("s_idx"), sem("s_m"), sem("s_t"), sem("s_mt"),
                                               sem("s_qx"))
        s_mul, s_red, s_clip, s_exp, s_va, s_vd = (sem("s_mul"), sem("s_red"), sem("s_clip"), sem("s_exp"),
                                                   sem("s_va"), sem("s_vd"))
        s_seg, s_evc, s_evict, s_q = sem("s_seg"), sem("s_evc"), sem("s_evict"), sem("s_q")
        LOOKAHEAD, LAG = 3, 3

        def pipeline(eng, step):
            for q in range(-LOOKAHEAD, RING):
                step(q, q % RING, 1)
            with eng.Fori(1, ROUNDS - 1) as i:
                for s in range(RING):
                    step(i * RING + s, s, i + 1)
            for q in range((ROUNDS - 1) * RING, PAIRS + LAG):
                step(q, q % RING, q // RING + 1)

        def there(q):
            return not isinstance(q, int) or 0 <= q < PAIRS

        def heads(ap):
            return ap.rearrange("p a (h d) -> p a h d", d=D_HEAD)

        with nc.Block() as block:
            @block.sync
            def _(sp):
                def load(t):
                    sp.dma_start(q_tile[:, bass.ds(t % 2, 1), :].rearrange("p a n -> p (a n)"),
                                 q_d[bass.ds(t * P, P), :]).then_inc(s_q, 16)
                load(0)
                sp.wait_ge(s_q, 16)
                load(1)
                with sp.Fori(2, TILES) as t:
                    used = sp.value_load(cnt_row[0:1, bass.ds(t - 2, 1)], min_val=1, max_val=VISITS)
                    wait_apart(sp, s_qx, used)
                    sp.wait_ge(s_q, 16 * t)
                    load(t)

            @block.gpsimd
            def _(pool):
                def gather(q, s):
                    wait(pool, s_seg, q - RING + 1)
                    pool.tensor_copy(idx[:, s, :], src_t[:, bass.ds(2 * q, 2)]).then_inc(s_idx, 1)
                    wait_apart(pool, s_idx, q + 1)
                    for u in range(2):
                        pool.indirect_dma_start(kv[:, s, u, :], None, kv_d,
                                                bass.IndirectOffsetOnAxis(idx[:, s, u:u + 1], 0),
                                                bounds_check=N_NODES - 1, oob_is_err=False
                                                ).then_inc(s_g[s][u], 16)
                for s in range(RING):
                    gather(s, s)
                with pool.Fori(1, ROUNDS) as i:
                    for s in range(RING):
                        gather(i * RING + s, s)
                for q in range(ROUNDS * RING, PAIRS):
                    gather(q, q % RING)

            @block.vector
            def _(dve):
                dve.memset(zeros[:, :], 0.0).then_inc(s_vd, 1)

                def step(q, s, fills):
                    a = q + LOOKAHEAD
                    sa, s1 = (s + LOOKAHEAD) % RING, (s - 1) % RING
                    if there(q):
                        for u in range(2):
                            dve.wait_ge(s_g[s][u], 16 * fills)
                            dve.wait_ge(s_qx, 2 * q + u + 1)
                            k = kv[:, s, u, 0:DIM]
                            dve.tensor_tensor(k, q_ps[:, (2 * s + u) % Q_BANKS, :], k, ALU.mult).then_inc(s_mul, 1)
                    if there(a):
                        wait(dve, s_seg, a - RING + 1)
                        dve.tensor_tensor(m_sb[:, sa, :, :], iota_row[:, :].unsqueeze(1).broadcast_to([P, 2, P]),
                                          loc_t[:, bass.ds(2 * a, 2)].unsqueeze(2).broadcast_to([P, 2, P]),
                                          ALU.is_equal).then_inc(s_m, 1)
                    if there(q):
                        dve.wait_ge(s_mul, 2 * q + 2)
                        dve.tensor_reduce(raw[:, s, :, :], heads(kv[:, s, :, 0:DIM]), AX.X, ALU.add).then_inc(s_red, 1)
                    if there(q - 1):
                        dve.wait_ge(s_exp, q)
                        v = heads(kv[:, s1, :, DIM:2 * DIM])[:, :, ACT_HEADS:, :]
                        w = score[:, s1, :, ACT_HEADS:].unsqueeze(3).broadcast_to(
                            [P, 2, HEADS - ACT_HEADS, D_HEAD])
                        dve.tensor_tensor(v, v, w, ALU.mult).then_inc(s_vd, 1)
                    if there(q):
                        dve.wait_ge(s_red, q + 1)
                        dve.tensor_scalar(raw[:, s, :, :], raw[:, s, :, :], -5.0, 5.0, ALU.max,
                                          ALU.min).then_inc(s_clip, 1)

                pipeline(dve, step)

            @block.scalar
            def _(act):
                act.memzero(idle[:, :]).then_inc(s_evict, 2)

                def evict(t):
                    par = t % 2
                    act.copy(agg[:, bass.ds(t, 1), 0:DIM], acc[:, bass.ds(par, 1), :])
                    act.copy(agg[:, bass.ds(t, 1), DIM:AGG], z_acc[:, bass.ds(par, 1), 0:HEADS]).then_inc(s_evc, 1)
                    wait_apart(act, s_evc, t + 1)
                    act.mul(acc[:, bass.ds(par, 1), :].bitcast(U32), acc[:, bass.ds(par, 1), :].bitcast(U32), 0.0)
                    z = z_acc[:, bass.ds(par, 1), 0:HEADS].bitcast(U32)
                    act.mul(z, z, 0.0).then_inc(s_evict, 1)

                def step(q, s, fills):
                    e, a = q - LAG, q + 2
                    sa = (s + 2) % RING
                    if there(e):
                        t0 = act.value_load(t_row[0:1, bass.ds(2 * e, 1)], min_val=0, max_val=TILES - 1)
                        t1 = act.value_load(t_row[0:1, bass.ds(2 * e + 2, 1)], min_val=0, max_val=TILES + 1)
                        with act.If(t1 > t0):
                            act.wait_ge(s_seg, e + 1)
                            evict(t0)
                            with act.If(t1 > t0 + 1):
                                evict((t0 + 1).with_bounds(min_val=1, max_val=TILES - 1))
                    if there(a):
                        act.wait_ge(s_t, a + 1)
                        act.copy(mt_sb[:, sa, :, :], t_ps[:, 0, 0:2 * P].rearrange("p (a n) -> p a n", a=2)).then_inc(s_mt, 1)
                    if there(q):
                        act.wait_ge(s_clip, q + 1)
                        act.activation(score[:, s, :, :], raw[:, s, :, :], ACT.Exp).then_inc(s_exp, 1)
                        act.wait_ge(s_exp, q + 1)
                        for u in range(2):
                            for h in range(ACT_HEADS):
                                v = kv[:, s, u, DIM + h * D_HEAD:DIM + (h + 1) * D_HEAD]
                                last = act.activation(v, v, ACT.Copy, scale=score[:, s, u, h:h + 1])
                        last.then_inc(s_va, 1)
                pipeline(act, step)

            @block.tensor
            def _(pe):
                pe.wait_ge(s_vd, 1)
                for par in range(2):
                    pe.matmul(acc[:, par, :], zeros[:, 0:P], zeros[:, :], start=True, stop=True)
                    last = pe.matmul(z_acc[:, par, 0:HEADS], zeros[:, 0:P], zeros[:, 0:HEADS], start=True, stop=True)
                last.then_inc(s_init, 1)

                def step(q, s, fills):
                    a, b, c = q + 3, q + 1, q - 2
                    sa, sb_, sc = (s + 3) % RING, (s + 1) % RING, (s - 2) % RING
                    if there(b):
                        for u in range(2):
                            t = pe.value_load(t_row[0:1, bass.ds(2 * b + u, 1)], min_val=0, max_val=TILES - 1)
                            pe.wait_ge(s_mt, b + 1)
                            wait(pe, s_mul, 2 * b + u + 1 - Q_BANKS)
                            pe.wait_ge(s_q, 16 * (t + 1))
                            for n in range(3):
                                last = pe.matmul(q_ps[:, (2 * sb_ + u) % Q_BANKS, :], mt_sb[:, sb_, u, :],
                                                 q_tile[:, bass.ds(t % 2, 1), n * DIM:(n + 1) * DIM],
                                                 start=(n == 0), stop=(n == 2))
                            last.then_inc(s_qx, 1)
                    if there(c):
                        wait_apart(pe, s_va, c + 1)
                        pe.wait_ge(s_vd, c + 2)
                        for u in range(2):
                            t = pe.value_load(t_row[0:1, bass.ds(2 * c + u, 1)], min_val=0, max_val=TILES - 1)
                            pe.wait_ge(s_evict, t + 1)
                            pe.matmul(acc[:, bass.ds(t % 2, 1), :], m_sb[:, sc, u, :],
                                      kv[:, sc, u, DIM:2 * DIM], start=False, stop=True, skip_group_check=True)
                            last = pe.matmul(z_acc[:, bass.ds(t % 2, 1), 0:HEADS], m_sb[:, sc, u, :],
                                             score[:, sc, u, :], start=False, stop=True, skip_group_check=True)
                        last.then_inc(s_seg, 1)
                    if there(a):
                        pe.wait_ge(s_m, a + 1)
                        wait(pe, s_mt, a)
                        for u in range(2):
                            last = pe.transpose(t_ps[:, 0, u * P:(u + 1) * P], m_sb[:, sa, u, :], ident[:, :])
                        last.then_inc(s_t, 1)
                pipeline(pe, step)


def normalise(nc, x, gamma, beta, out, agg):
    with ExitStack() as ctx:
        def sb(name, shape, dt):
            return ctx.enter_context(nc.sbuf_tensor(name, shape, dt))

        def sem(name):
            return ctx.enter_context(nc.semaphore(name))

        x_sb = sb("x_res", [P, 2, DIM], F32)
        rz = sb("rz", [P, TILES, HEADS], F32)
        gam, bet = sb("gam", [P, DIM], F32), sb("bet", [P, DIM], F32)
        mean, amp = sb("mean", [P, DIM], F32), sb("amp", [P, DIM], F32)
        ones, ones_last = sb("ones", [P, P], F32), sb("ones_last", [P, P], F32)
        sq = sb("sq", [P, 2, DIM], F32)
        y = sb("y", [P, 2, DIM], F32)
        stats = sb("stats", [P, 2, 6], F32)
        mv = sb("mv", [P, 2, 2], F32)
        std, rstd, shift = sb("std", [P, 2, 1], F32), sb("rstd", [P, 2, 1], F32), sb("shift", [P, 2, 1], F32)
        o_sb = sb("o_sb", [P, 2, DIM], F32)
        eps = sb("eps", [P, 1], F32)
        sum_ps = ctx.enter_context(nc.psum_tensor("sum_ps", [P, DIM], F32))
        var_ps = ctx.enter_context(nc.psum_tensor("var_ps", [P, DIM], F32))

        s_ld, s_par, s_one = [sem(f"s_ld{j}") for j in range(2)], sem("s_par"), sem("s_one")
        s_rz, s_h, s_hx, s_hd, s_sum = sem("s_rz"), sem("s_h"), sem("s_hx"), sem("s_hd"), sem("s_sum")
        s_mean, s_d, s_sq, s_var, s_amp = sem("s_mean"), sem("s_d"), sem("s_sq"), sem("s_var"), sem("s_amp")
        s_xb, s_y, s_yx, s_st, s_mv, s_std = (sem("s_xb"), sem("s_y"), sem("s_yx"), sem("s_st"), sem("s_mv"),
                                              sem("s_std"))
        s_rs, s_sh, s_o = sem("s_rs"), sem("s_sh"), sem("s_o")
        s_out = [sem(f"s_out{j}") for j in range(2)]
        HALF = (TILES - 1) // 2

        def row(t):
            return agg[:, bass.ds(t, 1), 0:DIM].rearrange("p a n -> p (a n)")

        def tiles(eng, step, head=0):
            for i in range(head):
                for j in range(2):
                    step(2 * i + j, j, i)
            with eng.Fori(head, HALF) as i:
                for j in range(2):
                    step(2 * i + j, j, i)
            step(TILES - 1, 0, HALF)

        with nc.Block() as block:
            @block.sync
            def _(sp):
                sp.dma_start(gam[:, :], gamma.broadcast_to([P, DIM])).then_inc(s_par, 16)
                sp.dma_start(bet[:, :], beta.broadcast_to([P, DIM])).then_inc(s_par, 16)

                def first(t, j, i):
                    wait(sp, s_hx if j else s_hd, i)
                    sp.dma_start(x_sb[:, j, :], x[bass.ds(t * P, P), :]).then_inc(s_ld[j], 16)
                tiles(sp, first, 1)
                sp.wait_ge(s_hd, HALF + 1)
                sp.wait_ge(s_hx, HALF)

                def second(t, j, i):
                    wait(sp, s_xb, t - 1)
                    sp.dma_start(x_sb[:, j, :], x[bass.ds(t * P, P), :]).then_inc(s_ld[j], 16)
                tiles(sp, second, 1)

            @block.gpsimd
            def _(pool):
                pool.memset(ones[:, :], 1.0)
                pool.memset(ones_last[:, :], 1.0).then_inc(s_one, 1)
                pool.wait_ge(s_one, 1)
                pool.affine_select(out=ones_last[:, :], in_=ones_last[:, :], compare_op=ALU.is_ge, fill=0.0,
                                   base=LAST_ROWS - 1, pattern=[[0, P]], channel_multiplier=-1).then_inc(s_one, 1)

                with pool.Fori(0, HALF) as i:
                    pool.wait_ge(s_ld[1], 16 * (i + 1))
                    pool.wait_ge(s_h, 2 * i + 2)
                    pool.tensor_tensor(row(2 * i + 1), row(2 * i + 1), x_sb[:, 1, :], ALU.add).then_inc(s_hx, 1)

                pool.wait_ge(s_par, 32)

                def x_beta(t, j, i):
                    pool.wait_ge(s_ld[j], 16 * (i + HALF + 2 - j))
                    wait(pool, s_yx, t - 1)
                    pool.tensor_tensor(sq[:, j, :], x_sb[:, j, :], bet[:, :], ALU.add).then_inc(s_xb, 1)
                pool.wait_ge(s_var, TILES)
                tiles(pool, x_beta, 1)

            @block.tensor
            def _(pe):
                pe.wait_ge(s_one, 2)
                pe.wait_ge(s_rz, 3)
                for ps in (sum_ps, var_ps):
                    pe.matmul(ps[:, :], ones[:, :], sq[:, 0, :], start=True, stop=True).then_inc(s_sum, 1)

                def colsum(t, j, i):
                    pe.wait_ge(s_hx if j else s_hd, i + 1)
                    w = ones_last if isinstance(t, int) and t == TILES - 1 else ones
                    pe.matmul(sum_ps[:, :], w[:, :], row(t), start=False, stop=True,
                              skip_group_check=True).then_inc(s_sum, 1)
                tiles(pe, colsum)

                def colsquare(t, j, i):
                    pe.wait_ge(s_sq, t + 1)
                    w = ones_last if isinstance(t, int) and t == TILES - 1 else ones
                    pe.matmul(var_ps[:, :], w[:, :], sq[:, j, :], start=False, stop=True,
                              skip_group_check=True).then_inc(s_var, 1)
                tiles(pe, colsquare)

            @block.scalar
            def _(act):
                act.wait_ge(s_sum, TILES + 2)
                act.mul(mean[:, :], sum_ps[:, :], 1.0 / N_NODES).then_inc(s_mean, 1)

                def square(t, j, i):
                    act.wait_ge(s_d, t + 1)
                    wait(act, s_var, t - 1)
                    act.activation(sq[:, j, :], row(t), ACT.Square).then_inc(s_sq, 1)
                tiles(act, square, 1)
                act.wait_ge(s_var, TILES)
                act.wait_ge(s_rz, 4)
                act.activation(amp[:, :], var_ps[:, :], ACT.Sqrt, scale=1.0 / N_NODES,
                               bias=eps[:, 0:1]).then_inc(s_amp, 1)

                def norm(t, j, i):
                    if not isinstance(t, int) or t < TILES:
                        act.wait_ge(s_mv, t + 1)
                        wait(act, s_sh, t - 1)
                        act.activation(std[:, j, :], mv[:, j, 1:2], ACT.Sqrt, bias=eps[:, 0:1]).then_inc(s_std, 1)
                    if not isinstance(t, int) or t > 0:
                        jj = 1 - j
                        act.wait_ge(s_sh, t)
                        wait(act, s_out[jj], 16 * (i - jj))
                        act.activation(o_sb[:, jj, :], y[:, jj, :], ACT.Identity, scale=rstd[:, jj, :],
                                       bias=shift[:, jj, :]).then_inc(s_o, 1)
                        act.wait_ge(s_o, t)
                        act.dma_start(out[bass.ds((t - 1) * P, P), :], o_sb[:, jj, :]).then_inc(s_out[jj], 16)
                tiles(act, norm, 1)
                norm(TILES, 1, HALF)
                act.wait_ge(s_out[0], 16 * (HALF + 1))
                act.wait_ge(s_out[1], 16 * HALF)

            @block.vector
            def _(dve):
                dve.memset(eps[:, :], 1e-5)
                dve.memset(sq[:, :, :], 0.0)
                dve.tensor_scalar(rz[:, :, :], agg[:, :, DIM:AGG], 1e-6, None, ALU.add).then_inc(s_rz, 1)
                dve.wait_ge(s_rz, 1)
                dve.reciprocal(rz[:, :, :], rz[:, :, :]).then_inc(s_rz, 3)
                dve.wait_ge(s_rz, 4)

                def h_of(t, j, i):
                    h = row(t).rearrange("p (h d) -> p h d", d=D_HEAD)
                    r = rz[:, bass.ds(t, 1), :].rearrange("p a h -> p (a h)").unsqueeze(2).broadcast_to(
                        [P, HEADS, D_HEAD])
                    dve.tensor_tensor(h, h, r, ALU.mult).then_inc(s_h, 1)
                    if j == 0:
                        dve.wait_ge(s_h, t + 1)
                        dve.wait_ge(s_ld[0], 16 * (i + 1))
                        dve.tensor_tensor(row(t), row(t), x_sb[:, 0, :], ALU.add).then_inc(s_hd, 1)
                tiles(dve, h_of)
                dve.wait_ge(s_mean, 1)

                def centre(t, j, i):
                    dve.tensor_tensor(row(t), row(t), mean[:, :], ALU.subtract).then_inc(s_d, 1)
                tiles(dve, centre)
                dve.wait_ge(s_amp, 1)
                dve.reciprocal(amp[:, :], amp[:, :]).then_inc(s_amp, 1)
                dve.wait_ge(s_amp, 2)
                dve.wait_ge(s_par, 32)
                dve.tensor_tensor(amp[:, :], amp[:, :], gam[:, :], ALU.mult).then_inc(s_amp, 1)
                dve.wait_ge(s_amp, 3)

                def line(t, j, i):
                    inside = not isinstance(t, int) or t < TILES
                    if inside:
                        wait(dve, s_o, t - 1)
                        dve.tensor_tensor(y[:, j, :], row(t), amp[:, :], ALU.mult).then_inc(s_y, 1)
                    if not isinstance(t, int) or t > 0:
                        jj = 1 - j
                        dve.wait_ge(s_std, t)
                        dve.reciprocal(rstd[:, jj, :], std[:, jj, :]).then_inc(s_rs, 1)
                        dve.wait_ge(s_rs, t)
                        dve.scalar_tensor_tensor(out=shift[:, jj, :], in0=mv[:, jj, 0:1], scalar=-1.0,
                                                 in1=rstd[:, jj, :], op0=ALU.mult,
                                                 op1=ALU.mult).then_inc(s_sh, 1)
                    if inside:
                        dve.wait_ge(s_y, t + 1)
                        dve.wait_ge(s_xb, t + 1)
                        dve.tensor_tensor(y[:, j, :], y[:, j, :], sq[:, j, :], ALU.add).then_inc(s_yx, 1)
                        dve.wait_ge(s_yx, t + 1)
                        dve.bn_stats(stats[:, j, :], y[:, j, :]).then_inc(s_st, 1)
                        wait_apart(dve, s_st, t + 1)
                        dve.bn_aggr(mv[:, j, :], stats[:, j, :]).then_inc(s_mv, 1)
                tiles(dve, line, 1)
                line(TILES, 1, HALF)


def program(nc, xT, x, wq, wk, wv, gamma, beta, edges, dlast, out):
    kv_d = nc.dram_tensor("kv_d", (ROWS, 2 * DIM), F32, kind="Internal").ap()
    q_d = nc.dram_tensor("q_d", (ROWS, 3 * DIM), BF16, kind="Internal").ap()
    t_d = nc.dram_tensor("t_d", (VCOLS,), I32, kind="Internal").ap()
    cnt_d = nc.dram_tensor("cnt_d", (64,), I32, kind="Internal").ap()
    with ExitStack() as ctx:
        def sb(name, shape, dt):
            return ctx.enter_context(nc.sbuf_tensor(name, shape, dt))

        tabs = (sb("src_t", [P, VCOLS], I32),
                sb("loc_t", [P, VCOLS], F32),
                sb("t_row", [1, VCOLS], I32),
                sb("cnt_row", [1, 64], I32),
                sb("iota_row", [P, P], F32),
                sb("ident", [P, P], F32),
                sb("kv", [P, RING, 2, 2 * DIM], F32))
        project(nc, xT, wq, wk, wv, edges, dlast, kv_d, q_d, t_d, cnt_d, tabs)
        agg = sb("agg", [P, TILES, AGG], F32)
        attend(nc, kv_d, q_d, tabs, agg)
        normalise(nc, x, gamma, beta, out, agg)


def kernel(**inputs):
    import numpy as np
    import concourse.bacc as bacc
    from concourse.bass_utils import run_bass_kernel_spmd

    x = np.zeros((ROWS, DIM), np.float32)
    x[:N_NODES] = inputs["x"]
    edges = np.zeros((BLOCKS_IN * P, 2), np.int32)
    edges[:N_EDGES, 0] = inputs["src"]
    edges[:N_EDGES, 1] = inputs["dst"]
    edges[N_EDGES:BLOCKS * P, 1] = ROWS - 1
    edges[BLOCKS * P:, 1] = -1
    arrays = {
        "xT": np.ascontiguousarray(x.reshape(TILES, P, CHUNKS, P).transpose(0, 3, 2, 1)),
        "x": x,
        "wq": np.ascontiguousarray(inputs["L0_gnn_Wq"]),
        "wk": np.ascontiguousarray(inputs["L0_gnn_Wk"]),
        "wv": np.ascontiguousarray(inputs["L0_gnn_Wv"]),
        "gamma": np.ascontiguousarray(inputs["L0_gnn_bn_gamma"]).reshape(1, DIM),
        "beta": np.ascontiguousarray(inputs["L0_gnn_bn_beta"]).reshape(1, DIM),
        "edges": np.ascontiguousarray(edges.reshape(BLOCKS_IN, P, 2).transpose(0, 2, 1)).reshape(BLOCKS_IN, 2 * P),
        "dlast": np.ascontiguousarray(edges[P - 1::P, 1]).reshape(1, BLOCKS_IN),
    }
    nc = bacc.Bacc("TRN2", target_bir_lowering=False, num_devices=1)
    aps = {}
    for name, a in arrays.items():
        aps[name] = nc.dram_tensor(f"in_{name}", a.shape, mybir.dt.from_np(a.dtype), kind="ExternalInput").ap()
    out = nc.dram_tensor("out_rows", (ROWS, DIM), F32, kind="ExternalOutput").ap()
    program(nc, out=out, **aps)
    got = run_bass_kernel_spmd(nc, [{f"in_{n}": a for n, a in arrays.items()}], core_ids=[0])
    return got.results[0]["out_rows"][:N_NODES]
```

```python
from contextlib import ExitStack

import concourse.bass as bass
from concourse import mybir

F32 = mybir.dt.float32
BF16 = mybir.dt.bfloat16
I32 = mybir.dt.int32
F32R = mybir.dt.float32r
U32 = mybir.dt.uint32
ALU = mybir.AluOpType
ACT = mybir.ActivationFunctionType
AX = mybir.AxisListType

P = 128
N_NODES, DIM, HEADS = 6250, 512, 8
D_HEAD = DIM // HEADS
N_EDGES = 106250
TILES = -(-N_NODES // P)
ROWS = TILES * P
BLOCKS = -(-N_EDGES // P)
BLOCKS_IN = BLOCKS + 1
STAIRS = BLOCKS + TILES - 1
PAIRS = -(-STAIRS // 2)
VISITS = 2 * PAIRS
VTILES = -(-(VISITS + 1) // P)
VCOLS = VTILES * P
RING = 9
ROUNDS = PAIRS // RING
MT_RING = 3
Q_BANKS = 3
CHUNKS = DIM // P
SKIP = 65536.0
SLOTS = 8
DEPTH = 4
ACT_HEADS = 5
POOL_HEADS = 1
AGG = DIM + 2 * HEADS
VBODY = 2 * RING
MASKS = -(-(VISITS + VBODY - 2) // VBODY)
LAST_ROWS = N_NODES - (TILES - 1) * P


def bit_of(visit):
    return divmod(visit + VBODY - 2, VBODY)


def wait(eng, sem, value):
    if not (isinstance(value, int) and value <= 0):
        eng.wait_ge(sem, value)


def wait_apart(eng, sem, value):
    if not isinstance(value, int):
        value = eng.snap(eng.to_reg(value))
        eng.wait_ge(sem, 1)
    wait(eng, sem, value)


def project(nc, xT, wq, wk, wv, edges, dlast, kv_d, q_d, t_d, cnt_d, tabs):
    src_t, loc_t, bits_row, cnt_row, iota_row, ident = tabs
    with ExitStack() as ctx:
        def sb(name, shape, dt):
            return ctx.enter_context(nc.sbuf_tensor(name, shape, dt))

        def sem(name):
            return ctx.enter_context(nc.semaphore(name))

        w_sb = sb("w_sb", [P, 3, CHUNKS, DIM], F32)
        x_sb = [sb(f"x_sb{j}", [P, CHUNKS, P], F32) for j in range(2)]
        kv_sb = [sb(f"kv_sb{j}", [P, 2 * DIM], F32) for j in range(2)]
        q_sb = [sb(f"q_sb{j}", [P, 2, DIM], F32) for j in range(2)]
        kv_ps = [ctx.enter_context(nc.psum_tensor(f"kv_ps{j}", [P, 2 * DIM], F32)) for j in range(2)]
        q_ps = [ctx.enter_context(nc.psum_tensor(f"q_ps{j}", [P, DIM], F32)) for j in range(2)]
        tab_ps = ctx.enter_context(nc.psum_tensor("tab_ps", [P, 2, 512], F32))
        dl = sb("dl", [P, BLOCKS_IN], I32)
        k128 = sb("k128", [P, BLOCKS_IN], I32)
        ends = sb("ends", [P, BLOCKS_IN], F32)
        below = sb("below", [P, VCOLS], F32)
        v128i = sb("v128i", [P, VTILES], I32)
        v128 = sb("v128", [P, VTILES], F32)
        kf = sb("kf", [P, VTILES], F32)
        ki = sb("ki", [P, VTILES], I32)
        t128 = sb("t128", [P, VTILES], F32)
        ti = sb("ti", [P, VTILES], I32)
        rows = sb("rows", [P, VTILES, 2 * P], I32)
        loc = sb("loc", [P, VCOLS], F32)
        srcf = sb("srcf", [P, VCOLS], F32)
        skip = sb("skip", [P, VCOLS], F32)
        iota_i = sb("iota_i", [P, P], I32)
        col_i = sb("col_i", [P, 1], I32)
        col = sb("col", [P, 1], F32)
        t_bc = sb("t_bc", [64, VCOLS], I32)
        t_row = sb("t_row", [1, VCOLS], I32)
        steps = sb("steps", [1, MASKS * VBODY], F32)
        powers = sb("powers", [1, VBODY], F32)
        masks = sb("masks", [1, MASKS], F32)
        cnt = sb("cnt", [64, 1], F32)
        cnti = sb("cnti", [64, 1], I32)

        s_w = sem("s_w")
        s_x = [sem(f"s_x{j}") for j in range(2)]
        s_kvst = [sem(f"s_kvst{j}") for j in range(2)]
        s_qst = [sem(f"s_qst{j}") for j in range(2)]
        s_proj, s_kvc = sem("s_proj"), sem("s_kvc")
        s_qh, s_ql = sem("s_qh"), sem("s_ql")
        s_dl, s_iota, s_tab, s_rows = sem("s_dl"), sem("s_iota"), sem("s_tab"), sem("s_rows")
        s_visit, s_tr, s_trc, s_td, s_tb, s_cnt = (sem("s_visit"), sem("s_tr"), sem("s_trc"), sem("s_td"),
                                                   sem("s_tb"), sem("s_cnt"))
        cuts = [0, 8, 16, (TILES - 1) // 2]

        def tiles(eng, part, step):
            with eng.Fori(cuts[part], cuts[part + 1]) as i:
                for j in range(2):
                    step(i, j)

        with nc.Block() as block:
            @block.sync
            def _(sp):
                for n, w in enumerate((wq, wk, wv)):
                    sp.dma_start(w_sb[:, n, :, :], w.rearrange("(c p) n -> p c n", p=P)).then_inc(s_w, 16)
                for j in range(2):
                    sp.dma_start(x_sb[j][:, :, :], xT[j]).then_inc(s_x[j], 16)

                def step(i, j, more=True):
                    tile = 2 * i + j
                    if more:
                        sp.wait_ge(s_proj, tile + 1)
                        sp.dma_start(x_sb[j][:, :, :], xT[bass.ds(tile + 2, 1)].rearrange("a p c n -> (a p) c n")
                                     if not isinstance(tile, int) else xT[tile + 2]).then_inc(s_x[j], 16)
                    sp.wait_ge(s_ql, tile + 1)
                    sp.dma_start(q_d[bass.ds(tile * P, P), :],
                                 q_sb[j][:, :, :].rearrange("p a n -> p (a n)")).then_inc(s_qst[j], 16)
                with sp.Fori(0, cuts[3] - 1) as i:
                    for j in range(2):
                        step(i, j)
                step(cuts[3] - 1, 0)
                step(cuts[3] - 1, 1, False)
                step(cuts[3], 0, False)
                for j in range(2):
                    sp.wait_ge(s_qst[j], 16 * (cuts[3] + 1 - j))
                    sp.wait_ge(s_kvst[j], 16 * (cuts[3] + 1 - j))

            @block.gpsimd
            def _(pool):
                pool.dma_start(dl[:, :], dlast.broadcast_to([P, BLOCKS_IN])).then_inc(s_dl, 16)
                pool.iota(k128[:, :], pattern=[[P, BLOCKS_IN]], base=0, channel_multiplier=0)
                pool.iota(v128i[:, :], pattern=[[P * P, VTILES]], base=0, channel_multiplier=P)
                pool.iota(col_i[:, :], pattern=[[1, 1]], base=0, channel_multiplier=1)
                pool.iota(iota_i[:, :], pattern=[[1, P]], base=0, channel_multiplier=0).then_inc(s_iota, 1)
                pool.wait_ge(s_visit, 1)
                for a in range(VTILES):
                    pool.indirect_dma_start(rows[:, a, :], None, edges,
                                            bass.IndirectOffsetOnAxis(ki[:, a:a + 1], 0),
                                            bounds_check=BLOCKS_IN - 1, oob_is_err=False).then_inc(s_rows, 16)
                pool.dma_start(t_d.rearrange("(a p) -> p a", p=P), ti[:, :], allow_slow_non_contiguous=True).then_inc(s_td, 16)
                pool.wait_ge(s_td, 16)
                pool.dma_start(t_row[:, :], t_d.rearrange("(a n) -> a n", a=1)).then_inc(s_tb, 16)
                pool.dma_start(t_bc[:, :], t_d.rearrange("(a n) -> a n", a=1).broadcast_to([64, VCOLS])
                               ).then_inc(s_tb, 16)
                pool.wait_ge(s_cnt, 3)
                pool.dma_start(cnt_d.rearrange("(p a) -> p a", a=1), cnti[:, :], allow_slow_non_contiguous=True).then_inc(s_td, 16)
                pool.wait_ge(s_td, 32)
                pool.dma_start(cnt_row[:, :], cnt_d.rearrange("(a n) -> a n", a=1)).then_inc(s_tb, 16)
                pool.wait_ge(s_tb, 48)

            @block.tensor
            def _(pe):
                pe.wait_ge(s_w, 48)

                def step(i, j):
                    tile = 2 * i + j
                    pe.wait_ge(s_x[j], 16 * (i + 1))
                    wait(pe, s_kvc, tile - 1)
                    wait(pe, s_ql, tile - 1)
                    for n, out in enumerate((q_ps[j][:, :], kv_ps[j][:, 0:DIM], kv_ps[j][:, DIM:2 * DIM])):
                        for c in range(CHUNKS):
                            last = pe.matmul(out, x_sb[j][:, c, :], w_sb[:, n, c, :],
                                             start=(c == 0), stop=(c == CHUNKS - 1))
                    last.then_inc(s_proj, 1)
                for j in range(2):
                    step(0, j)
                with pe.Fori(1, cuts[1]) as i:
                    for j in range(2):
                        step(i, j)
                tiles(pe, 1, step)
                pe.wait_ge(s_visit, 3)
                for n, tab in enumerate((srcf, loc)):
                    if n:
                        pe.wait_ge(s_trc, 1)
                    for a in range(VTILES):
                        last = pe.transpose(tab_ps[:, a // 4, (a % 4) * P:(a % 4 + 1) * P],
                                            tab[:, a * P:(a + 1) * P], ident[:, :])
                    last.then_inc(s_tr, 1)
                tiles(pe, 2, step)
                step(cuts[3], 0)

            @block.scalar
            def _(act):
                def step(i, j):
                    tile = 2 * i + j
                    act.wait_ge(s_proj, tile + 1)
                    wait(act, s_kvst[j], 16 * i)
                    act.copy(kv_sb[j][:, :], kv_ps[j][:, :]).then_inc(s_kvc, 1)
                    act.wait_ge(s_kvc, tile + 1)
                    act.dma_start(kv_d[bass.ds(tile * P, P), :], kv_sb[j][:, :]).then_inc(s_kvst[j], 16)
                for j in range(2):
                    step(0, j)
                with act.Fori(1, cuts[3]) as i:
                    for j in range(2):
                        step(i, j)
                step(cuts[3], 0)

            @block.vector
            def _(dve):
                n_tab = [0]

                def tab(ins):
                    ins.then_inc(s_tab, 1)
                    n_tab[0] += 1
                    dve.wait_ge(s_tab, n_tab[0])

                dve.wait_ge(s_iota, 1)
                dve.wait_ge(s_dl, 16)
                tab(dve.tensor_copy(iota_row[:, :], iota_i[:, :]))
                tab(dve.tensor_copy(col[:, :], col_i[:, :]))
                tab(dve.tensor_scalar(ident[:, :], iota_row[:, :], col[:, 0:1], None, ALU.is_equal))
                tab(dve.tensor_copy(v128[:, :], v128i[:, :]))
                tab(dve.tensor_tensor(ends[:, :], dl[:, :], k128[:, :], ALU.add))
                for a in range(VTILES):
                    tab(dve.tensor_scalar(below[:, 0:BLOCKS], ends[:, 0:BLOCKS], v128[:, a:a + 1], None,
                                          ALU.is_lt))
                    tab(dve.tensor_reduce(kf[:, a:a + 1], below[:, 0:BLOCKS], AX.X, ALU.add))
                tab(dve.tensor_copy(ki[:, :], kf[:, :]))
                tab(dve.tensor_scalar(kf[:, :], kf[:, :], float(P), None, ALU.mult))
                tab(dve.tensor_tensor(t128[:, :], v128[:, :], kf[:, :], ALU.subtract))
                dve.tensor_scalar(ti[:, :], t128[:, :], 1.0 / P, None, ALU.mult).then_inc(s_visit, 1)

                def step(i, j):
                    tile = 2 * i + j
                    dve.wait_ge(s_proj, tile + 1)
                    wait(dve, s_qst[j], 16 * i)
                    hi, lo = (q_sb[j][:, n, :] for n in range(2))
                    dve.tensor_scalar(hi.bitcast(F32R), q_ps[j][:, :], D_HEAD ** -0.5, None,
                                      ALU.mult).then_inc(s_qh, 1)
                    dve.wait_ge(s_qh, tile + 1)
                    dve.scalar_tensor_tensor(out=lo.bitcast(F32R), in0=q_ps[j][:, :], scalar=D_HEAD ** -0.5,
                                             in1=hi, op0=ALU.mult, op1=ALU.subtract).then_inc(s_ql, 1)
                for j in range(2):
                    step(0, j)
                with dve.Fori(1, cuts[1]) as i:
                    for j in range(2):
                        step(i, j)
                dve.wait_ge(s_rows, 16 * VTILES)
                for a in range(VTILES):
                    last = dve.tensor_scalar(loc[:, a * P:(a + 1) * P], rows[:, a, P:2 * P],
                                             t128[:, a:a + 1], None, ALU.subtract)
                tab(last)
                tab(dve.tensor_scalar(skip[:, :], loc[:, :], 0.0, SKIP, ALU.is_lt, ALU.mult))
                tab(dve.tensor_tensor(srcf[:, :].rearrange("p (a n) -> p a n", n=P), rows[:, :, 0:P],
                                      skip[:, :].rearrange("p (a n) -> p a n", n=P), ALU.add))
                tab(dve.tensor_scalar(skip[:, :], loc[:, :], float(P - 1), SKIP, ALU.is_gt, ALU.mult))
                tab(dve.tensor_tensor(srcf[:, :], srcf[:, :], skip[:, :], ALU.add))
                dve.tensor_copy(srcf[0:2 * RING, 0:P], rows[0:2 * RING, 0, 0:P]).then_inc(s_visit, 2)
                tab(dve.memset(powers[:, :], 1.0))
                tab(dve.memset(steps[:, :], 0.0))
                dve.wait_ge(s_tb, 32)
                n = 1
                while n < VBODY:
                    m = min(n, VBODY - n)
                    tab(dve.tensor_scalar(powers[:, n:n + m], powers[:, 0:m], float(2 ** n), None, ALU.mult))
                    n += m
                last_v = MASKS * VBODY - (VBODY - 2) - 1
                last_v = min(last_v, VISITS)
                tab(dve.tensor_tensor(steps[:, VBODY - 1:VBODY - 1 + last_v], t_row[:, 1:last_v + 1],
                                      t_row[:, 0:last_v], ALU.subtract))
                by_mask = steps[:, :].rearrange("p (m k) -> p m k", k=VBODY)
                tab(dve.tensor_tensor(by_mask, by_mask, powers[:, :].unsqueeze(1).broadcast_to([1, MASKS, VBODY]),
                                      ALU.mult))
                tab(dve.tensor_reduce(masks[:, :], by_mask, AX.X, ALU.add))
                tab(dve.tensor_copy(bits_row[:, :], masks[:, :]))
                dve.tensor_scalar(below[0:64, :], t_bc[:, :], col[0:64, 0:1], None,
                                  ALU.is_le).then_inc(s_cnt, 1)
                dve.wait_ge(s_cnt, 1)
                dve.tensor_reduce(cnt[:, :], below[0:64, :], AX.X, ALU.add).then_inc(s_cnt, 1)
                dve.wait_ge(s_cnt, 2)
                dve.tensor_copy(cnti[:, :], cnt[:, :]).then_inc(s_cnt, 1)
                tiles(dve, 1, step)
                half = tab_ps[:, :, :].rearrange("p a n -> p (a n)")[:, 0:VCOLS]
                dve.wait_ge(s_tr, 1)
                dve.tensor_copy(src_t[:, :], half).then_inc(s_trc, 1)
                dve.wait_ge(s_tr, 2)
                dve.tensor_copy(loc_t[:, :], half).then_inc(s_trc, 1)
                tiles(dve, 2, step)
                step(cuts[3], 0)


def attend(nc, kv_d, q_d, tabs, agg):
    src_t, loc_t, bits_row, cnt_row, iota_row, ident = tabs
    with ExitStack() as ctx:
        def sb(name, shape, dt):
            return ctx.enter_context(nc.sbuf_tensor(name, shape, dt))

        def ps(name, shape, dt):
            return ctx.enter_context(nc.psum_tensor(name, shape, dt))

        def sem(name):
            return ctx.enter_context(nc.semaphore(name))

        kv = sb("kv", [P, RING, 2, 2 * DIM], F32)
        idx = sb("idx", [P, RING, 2], I32)
        q_tile = sb("q_tile", [P, 2, 2 * DIM], F32)
        m_sb = sb("m_sb", [P, RING, 2, P], F32)
        mt_sb = sb("mt_sb", [P, MT_RING, 2 * P], F32R)
        raw = sb("raw", [P, RING, 2, HEADS], F32)
        score = sb("score", [P, RING, 2, HEADS], F32)
        zeros = sb("zeros", [P, DIM], BF16)
        idle = sb("idle", [P, 1], F32)
        acc = ps("acc", [P, 2, DIM], F32)
        parts = sb("parts", [P, RING, 2, 2 * HEADS], F32R)
        z_acc = ps("z_acc", [P, 2, DIM], F32)
        t_ps = ps("t_ps", [P, 8 * P], BF16)
        q_ps = ps("q_ps", [P, Q_BANKS, DIM], F32)

        s_g = [[sem(f"s_g{s}_{u}") for u in range(2)] for s in range(RING)]
        s_init, s_idx, s_m, s_t, s_mt, s_qx = (sem("s_init"), sem("s_idx"), sem("s_m"), sem("s_t"), sem("s_mt"),
                                               sem("s_qx"))
        s_mul, s_red, s_clip, s_exp, s_va, s_vd = (sem("s_mul"), sem("s_red"), sem("s_clip"), sem("s_exp"),
                                                   sem("s_va"), sem("s_vd"))
        s_seg, s_evc, s_evict, s_q = sem("s_seg"), sem("s_evc"), sem("s_evict"), sem("s_q")
        s_split, s_part = sem("s_split"), sem("s_part")
        SPLIT_LAG = 7
        LOOKAHEAD, LAG = 3, 3

        def pipeline(eng, step):
            for q in range(-LOOKAHEAD, RING):
                step(q, q % RING, 1)
            with eng.Fori(1, ROUNDS - 1) as i:
                for s in range(RING):
                    step(i * RING + s, s, i + 1)
            for q in range((ROUNDS - 1) * RING, PAIRS + LAG):
                step(q, q % RING, q // RING + 1)

        def there(q):
            return not isinstance(q, int) or 0 <= q < PAIRS

        def follow(eng, tiles):
            now, before = eng.alloc_register("mask_now"), eng.alloc_register("mask_before")
            regs = [eng.alloc_register(f"tile_{n}") for n in range(tiles)]
            for r in (now, *regs):
                eng.reg_mov(r, 0)

            def fetch(mask):
                eng.reg_mov(before, now)
                if not isinstance(mask, int) or mask < MASKS:
                    eng.reg_load(now, bits_row[0:1, bass.ds(mask, 1)])

            def bit(k, earlier=False):
                mask = eng.snap(before if earlier else now, min_val=0, max_val=2 ** VBODY - 1)
                return (mask >> k) & 1
            fetch(0)
            return regs, fetch, bit

        def as_bf16(ap):
            return ap.bitcast(BF16).rearrange("p (n h) -> p n h", h=2)[:, :, 1]

        def part(s, n):
            return parts[:, s, :, n * HEADS:(n + 1) * HEADS]

        def heads(ap):
            return ap.rearrange("p a (h d) -> p a h d", d=D_HEAD)

        with nc.Block() as block:
            @block.sync
            def _(sp):
                def load(t):
                    sp.dma_start(q_tile[:, bass.ds(t % 2, 1), :].rearrange("p a n -> p (a n)"),
                                 q_d[bass.ds(t * P, P), :]).then_inc(s_q, 16)
                load(0)
                sp.wait_ge(s_q, 16)
                load(1)
                with sp.Fori(2, TILES) as t:
                    used = sp.value_load(cnt_row[0:1, bass.ds(t - 2, 1)], min_val=1, max_val=VISITS)
                    wait_apart(sp, s_qx, used)
                    sp.wait_ge(s_q, 16 * t)
                    load(t)

            @block.gpsimd
            def _(pool):
                def index(q, s):
                    wait(pool, s_seg, q - RING + 1)
                    pool.tensor_copy(idx[:, s, :], src_t[:, bass.ds(2 * q, 2)]).then_inc(s_idx, 1)

                def gather(q, s, u):
                    if u == 0:
                        wait_apart(pool, s_idx, q + 1)
                    pool.indirect_dma_start(kv[:, s, u, :], None, kv_d,
                                            bass.IndirectOffsetOnAxis(idx[:, s, u:u + 1], 0),
                                            bounds_check=N_NODES - 1, oob_is_err=False
                                            ).then_inc(s_g[s][u], 16)

                def split_hi(p, s):
                    if there(p):
                        wait_apart(pool, s_exp, p + 1)
                        pool.tensor_copy(part(s, 0), score[:, s, :, :]).then_inc(s_split, 1)

                def split_lo(p, s):
                    if there(p):
                        wait_apart(pool, s_split, p + 1)
                        pool.tensor_tensor(part(s, 1), score[:, s, :, :], part(s, 0).bitcast(F32),
                                           ALU.subtract).then_inc(s_part, 1)

                def messages(p, s):
                    if there(p):
                        v = heads(kv[:, s, :, DIM:2 * DIM])[:, :, ACT_HEADS:ACT_HEADS + POOL_HEADS, :]
                        w = score[:, s, :, ACT_HEADS:ACT_HEADS + POOL_HEADS].unsqueeze(3).broadcast_to(
                            [P, 2, POOL_HEADS, D_HEAD])
                        pool.tensor_tensor(v, v, w, ALU.mult).then_inc(s_part, 1)

                def step(q, s):
                    p, sp = q - SPLIT_LAG, (s - SPLIT_LAG) % RING
                    if there(q):
                        index(q, s)
                    split_hi(p, sp)
                    if there(q):
                        gather(q, s, 0)
                    split_lo(p, sp)
                    if there(q):
                        gather(q, s, 1)
                    messages(p, sp)
                for s in range(RING):
                    step(s, s)
                with pool.Fori(1, ROUNDS) as i:
                    for s in range(RING):
                        step(i * RING + s, s)
                for q in range(ROUNDS * RING, PAIRS + SPLIT_LAG):
                    step(q, q % RING)

            @block.vector
            def _(dve):
                dve.memset(zeros[:, :], 0.0).then_inc(s_vd, 1)

                def step(q, s, fills):
                    a = q + LOOKAHEAD
                    sa, s1 = (s + LOOKAHEAD) % RING, (s - 1) % RING
                    if there(q):
                        for u in range(2):
                            dve.wait_ge(s_g[s][u], 16 * fills)
                            dve.wait_ge(s_qx, 2 * q + u + 1)
                            k = kv[:, s, u, 0:DIM]
                            dve.tensor_tensor(k, q_ps[:, (2 * s + u) % Q_BANKS, :], k, ALU.mult).then_inc(s_mul, 1)
                    if there(a):
                        wait(dve, s_seg, a - RING + 1)
                        dve.tensor_tensor(m_sb[:, sa, :, :].bitcast(F32R), iota_row[:, :].unsqueeze(1).broadcast_to([P, 2, P]),
                                          loc_t[:, bass.ds(2 * a, 2)].unsqueeze(2).broadcast_to([P, 2, P]),
                                          ALU.is_equal).then_inc(s_m, 1)
                    if there(q):
                        dve.wait_ge(s_mul, 2 * q + 2)
                        dve.tensor_reduce(raw[:, s, :, :], heads(kv[:, s, :, 0:DIM]), AX.X, ALU.add).then_inc(s_red, 1)
                    if there(q - 1):
                        dve.wait_ge(s_exp, q)
                        v = heads(kv[:, s1, :, DIM:2 * DIM])[:, :, ACT_HEADS + POOL_HEADS:, :]
                        w = score[:, s1, :, ACT_HEADS + POOL_HEADS:].unsqueeze(3).broadcast_to(
                            [P, 2, HEADS - ACT_HEADS - POOL_HEADS, D_HEAD])
                        dve.tensor_tensor(v, v, w, ALU.mult).then_inc(s_vd, 1)
                    if there(q):
                        dve.wait_ge(s_red, q + 1)
                        dve.tensor_scalar(raw[:, s, :, :], raw[:, s, :, :], -5.0, 5.0, ALU.max,
                                          ALU.min).then_inc(s_clip, 1)

                pipeline(dve, step)

            @block.scalar
            def _(act):
                act.memzero(idle[:, :]).then_inc(s_evict, 2)

                (tile_reg,), fetch, bit = follow(act, 1)

                def evict(t):
                    par = t % 2
                    act.copy(agg[:, bass.ds(t, 1), 0:DIM], acc[:, bass.ds(par, 1), :])
                    act.copy(agg[:, bass.ds(t, 1), DIM:AGG], z_acc[:, bass.ds(par, 1), 0:2 * HEADS]).then_inc(s_evc, 1)
                    wait_apart(act, s_evc, t + 1)
                    act.mul(acc[:, bass.ds(par, 1), :].bitcast(U32), acc[:, bass.ds(par, 1), :].bitcast(U32), 0.0)
                    z = z_acc[:, bass.ds(par, 1), 0:2 * HEADS].bitcast(U32)
                    act.mul(z, z, 0.0).then_inc(s_evict, 1)

                def step(q, s, fills):
                    e, a = q - LAG, q + 2
                    sa = (s + 2) % RING
                    if there(e):
                        t0 = act.snap(tile_reg, min_val=0, max_val=TILES - 1)
                        over = act.snap(sum(bit((2 * (s - LAG) + n + VBODY - 2) % VBODY,
                                                earlier=2 * (s - LAG) + n + VBODY - 2 < VBODY) for n in (1, 2)),
                                        min_val=0, max_val=2)
                        with act.If(over > 0):
                            act.wait_ge(s_seg, e + 1)
                            evict(t0)
                            with act.If(over > 1):
                                evict((t0 + 1).with_bounds(min_val=1, max_val=TILES - 1))
                        act.reg_mov(tile_reg, t0 + over)
                    if there(a):
                        act.wait_ge(s_t, a + 1)
                        act.copy(mt_sb[:, sa % MT_RING, :], t_ps[:, 0:2 * P]).then_inc(s_mt, 1)
                    if there(q):
                        act.wait_ge(s_clip, q + 1)
                        act.activation(score[:, s, :, :], raw[:, s, :, :], ACT.Exp).then_inc(s_exp, 1)
                        act.wait_ge(s_exp, q + 1)
                        for u in range(2):
                            for h in range(ACT_HEADS):
                                v = kv[:, s, u, DIM + h * D_HEAD:DIM + (h + 1) * D_HEAD]
                                last = act.activation(v, v, ACT.Copy, scale=score[:, s, u, h:h + 1])
                        last.then_inc(s_va, 1)
                    if s == RING - 1:
                        fetch(q // RING + 2 if isinstance(q, int) else fills + 1)
                pipeline(act, step)

            @block.tensor
            def _(pe):
                PLACES = RING
                tile_regs, fetch, bit = follow(pe, PLACES)
                pe.wait_ge(s_vd, 1)
                for par in range(2):
                    pe.matmul(acc[:, par, :], zeros[:, 0:P], zeros[:, :], start=True, stop=True)
                    last = pe.matmul(z_acc[:, par, 0:2 * HEADS], zeros[:, 0:P], zeros[:, 0:2 * HEADS], start=True, stop=True)
                last.then_inc(s_init, 1)

                def step(q, s, fills):
                    a, b, c = q + 3, q + 1, q - 2
                    sa, sb_, sc = (s + 3) % RING, (s + 1) % RING, (s - 2) % RING
                    if there(b):
                        for u in range(2):
                            v = 2 * sb_ + u
                            tile = pe.snap(pe.snap(tile_regs[(v - 1) % PLACES], min_val=0, max_val=TILES - 1)
                                           + bit(2 * s + u), min_val=0, max_val=TILES - 1)
                            pe.reg_mov(tile_regs[v % PLACES], tile)
                            pe.wait_ge(s_mt, b + 1)
                            wait(pe, s_mul, 2 * b + u + 1 - Q_BANKS)
                            pe.wait_ge(s_q, 16 * (tile + 1))
                            for n in range(2):
                                last = pe.matmul(q_ps[:, (2 * sb_ + u) % Q_BANKS, :], mt_sb[:, sb_ % MT_RING, u * P:(u + 1) * P],
                                                 q_tile[:, bass.ds(tile % 2, 1), n * DIM:(n + 1) * DIM].bitcast(F32R),
                                                 start=(n == 0), stop=(n == 1))
                            last.then_inc(s_qx, 1)
                    if there(c):
                        wait_apart(pe, s_va, c + 1)
                        pe.wait_ge(s_part, 2 * (c + 1))
                        pe.wait_ge(s_vd, c + 2)
                        for u in range(2):
                            tile = pe.snap(tile_regs[(2 * sc + u) % PLACES], min_val=0, max_val=TILES - 1)
                            pe.wait_ge(s_evict, tile + 1)
                            pe.matmul(acc[:, bass.ds(tile % 2, 1), :], m_sb[:, sc, u, :],
                                      kv[:, sc, u, DIM:2 * DIM], start=False, stop=True, skip_group_check=True)
                            last = pe.matmul(z_acc[:, bass.ds(tile % 2, 1), 0:2 * HEADS],
                                             m_sb[:, sc, u, :].bitcast(F32R), parts[:, sc, u, :], start=False,
                                             stop=True, skip_group_check=True)
                        last.then_inc(s_seg, 1)
                    if s == RING - 1:
                        fetch(q // RING + 2 if isinstance(q, int) else fills + 1)
                    if there(a):
                        pe.wait_ge(s_m, a + 1)
                        wait(pe, s_mt, a)
                        for u in range(2):
                            last = pe.transpose(t_ps[:, u * P:(u + 1) * P], as_bf16(m_sb[:, sa, u, :]), as_bf16(ident[:, :]))
                        last.then_inc(s_t, 1)
                pipeline(pe, step)


def normalise(nc, x, gamma, beta, out, agg):
    with ExitStack() as ctx:
        def sb(name, shape, dt):
            return ctx.enter_context(nc.sbuf_tensor(name, shape, dt))

        def sem(name):
            return ctx.enter_context(nc.semaphore(name))

        x_sb = sb("x_res", [P, SLOTS, DIM], F32)
        rz = sb("rz", [P, TILES, HEADS], F32)
        gam, bet = sb("gam", [P, DIM], F32), sb("bet", [P, DIM], F32)
        mean, amp = sb("mean", [P, DIM], F32), sb("amp", [P, DIM], F32)
        ones, ones_last = sb("ones", [P, P], F32), sb("ones_last", [P, P], F32)
        sq = sb("sq", [P, DEPTH, DIM], F32)
        y = sb("y", [P, DEPTH, DIM], F32)
        stats = sb("stats", [P, DEPTH, 6], F32)
        mv = sb("mv", [P, DEPTH, 2], F32)
        std, rstd, shift = (sb(name, [P, DEPTH, 1], F32) for name in ("std", "rstd", "shift"))
        o_sb = sb("o_sb", [P, DEPTH, DIM], F32)
        eps = sb("eps", [P, 1], F32)
        sum_ps = ctx.enter_context(nc.psum_tensor("sum_ps", [P, DIM], F32))
        var_ps = ctx.enter_context(nc.psum_tensor("var_ps", [P, DIM], F32))

        s_ld, s_par, s_one = [sem(f"s_ld{j}") for j in range(SLOTS)], sem("s_par"), sem("s_one")
        s_rz, s_h, s_hx, s_hd, s_sum = sem("s_rz"), sem("s_h"), sem("s_hx"), sem("s_hd"), sem("s_sum")
        s_mean, s_d, s_sq, s_var, s_amp = sem("s_mean"), sem("s_d"), sem("s_sq"), sem("s_var"), sem("s_amp")
        s_xb, s_y, s_yx, s_st, s_mv, s_std = (sem("s_xb"), sem("s_y"), sem("s_yx"), sem("s_st"), sem("s_mv"),
                                              sem("s_std"))
        s_rs, s_sh, s_o = sem("s_rs"), sem("s_sh"), sem("s_o")
        s_out = [sem(f"s_out{j}") for j in range(DEPTH)]
        BODIES = TILES // SLOTS
        assert BODIES * SLOTS == TILES - 1 and SLOTS % DEPTH == 0

        def row(t):
            return agg[:, bass.ds(t, 1), 0:DIM].rearrange("p a n -> p (a n)")

        def tiles(eng, step, ahead=0, behind=0):
            for t in range(ahead * SLOTS):
                step(t, t % SLOTS, t // SLOTS)
            with eng.Fori(ahead, BODIES) as i:
                for j in range(SLOTS):
                    step(i * SLOTS + j, j, i)
            for t in range(BODIES * SLOTS, TILES + behind):
                step(t, t % SLOTS, t // SLOTS)

        def there(t):
            return not isinstance(t, int) or 0 <= t < TILES

        def weights(t):
            return ones_last if isinstance(t, int) and t == TILES - 1 else ones

        with nc.Block() as block:
            @block.sync
            def _(sp):
                sp.dma_start(gam[:, :], gamma.broadcast_to([P, DIM])).then_inc(s_par, 16)
                sp.dma_start(bet[:, :], beta.broadcast_to([P, DIM])).then_inc(s_par, 16)

                def load(t, j, i, used):
                    for sem_used, n in used(t, j):
                        wait_apart(sp, sem_used, n)
                    sp.dma_start(x_sb[:, j, :], x[bass.ds(t * P, P), :]).then_inc(s_ld[j], 16)

                def first(t, j, i):
                    n = (i - 1) * (SLOTS // 2) + j // 2 + 1
                    load(t, j, i, lambda t, j: [(s_hx if j % 2 else s_hd, n)])
                tiles(sp, first, 1)
                sp.wait_ge(s_hd, TILES // 2 + 1)
                sp.wait_ge(s_hx, TILES // 2)

                def second(t, j, i):
                    load(t, j, i, lambda t, j: [(s_xb, t - SLOTS + 1)])
                tiles(sp, second, 1)

            @block.gpsimd
            def _(pool):
                pool.memset(ones[:, :], 1.0)
                pool.memset(ones_last[:, :], 1.0).then_inc(s_one, 1)
                pool.wait_ge(s_one, 1)
                pool.affine_select(out=ones_last[:, :], in_=ones_last[:, :], compare_op=ALU.is_ge, fill=0.0,
                                   base=LAST_ROWS - 1, pattern=[[0, P]], channel_multiplier=-1).then_inc(s_one, 1)

                def add_x(t, j, i):
                    if j % 2:
                        pool.wait_ge(s_ld[j], 16 * (i + 1))
                        pool.wait_ge(s_h, t + 1)
                        pool.tensor_tensor(row(t), row(t), x_sb[:, j, :], ALU.add).then_inc(s_hx, 1)
                tiles(pool, add_x)
                pool.wait_ge(s_par, 32)

                def x_beta(t, j, i):
                    d = j % DEPTH
                    pool.wait_ge(s_ld[j], 16 * (i + 1 + BODIES + (j == 0)))
                    wait(pool, s_yx, t - DEPTH + 1)
                    pool.tensor_tensor(sq[:, d, :], x_sb[:, j, :], bet[:, :], ALU.add).then_inc(s_xb, 1)
                pool.wait_ge(s_var, TILES)
                tiles(pool, x_beta, 1)

            @block.tensor
            def _(pe):
                pe.wait_ge(s_one, 2)
                pe.wait_ge(s_rz, 4)
                for ps in (sum_ps, var_ps):
                    pe.matmul(ps[:, :], ones[:, :], sq[:, 0, :], start=True, stop=True).then_inc(s_sum, 1)

                def colsum(t, j, i):
                    pe.wait_ge(s_hx if j % 2 else s_hd, i * (SLOTS // 2) + j // 2 + 1)
                    pe.matmul(sum_ps[:, :], weights(t)[:, :], row(t), start=False, stop=True,
                              skip_group_check=True).then_inc(s_sum, 1)
                tiles(pe, colsum)

                def colsquare(t, j, i):
                    pe.wait_ge(s_sq, t + 1)
                    pe.matmul(var_ps[:, :], weights(t)[:, :], sq[:, j % DEPTH, :], start=False, stop=True,
                              skip_group_check=True).then_inc(s_var, 1)
                tiles(pe, colsquare)

            @block.scalar
            def _(act):
                act.wait_ge(s_sum, TILES + 2)
                act.mul(mean[:, :], sum_ps[:, :], 1.0 / N_NODES).then_inc(s_mean, 1)

                def square(t, j, i):
                    act.wait_ge(s_d, t + 1)
                    wait(act, s_var, t - DEPTH + 1)
                    act.activation(sq[:, j % DEPTH, :], row(t), ACT.Square).then_inc(s_sq, 1)
                tiles(act, square, 1)
                act.wait_ge(s_var, TILES)
                act.activation(amp[:, :], var_ps[:, :], ACT.Sqrt, scale=1.0 / N_NODES,
                               bias=eps[:, 0:1]).then_inc(s_amp, 1)

                def norm(t, j, i):
                    a, b = (j - 1) % DEPTH, (j - 2) % DEPTH
                    if there(t - 1):
                        act.wait_ge(s_mv, t)
                        wait(act, s_sh, t - DEPTH)
                        act.activation(std[:, a, :], mv[:, a, 1:2], ACT.Sqrt, bias=eps[:, 0:1]).then_inc(s_std, 1)
                    if there(t - 2):
                        act.wait_ge(s_sh, t - 1)
                        wait(act, s_out[b], 16 * (i * (SLOTS // DEPTH) + (j - 2) // DEPTH))
                        act.activation(o_sb[:, b, :], y[:, b, :], ACT.Identity, scale=rstd[:, b, :],
                                       bias=shift[:, b, :]).then_inc(s_o, 1)
                        wait_apart(act, s_o, t - 1)
                        act.dma_start(out[bass.ds((t - 2) * P, P), :], o_sb[:, b, :]).then_inc(s_out[b], 16)
                tiles(act, norm, 1, 2)
                for d in range(DEPTH):
                    act.wait_ge(s_out[d], 16 * len(range(d, TILES, DEPTH)))

            @block.vector
            def _(dve):
                dve.memset(eps[:, :], 1e-5)
                dve.memset(sq[:, 0, :], 0.0)
                dve.scalar_tensor_tensor(out=rz[:, :, :], in0=agg[:, :, DIM + HEADS:AGG], scalar=1e-6,
                                         in1=agg[:, :, DIM:DIM + HEADS], op0=ALU.add, op1=ALU.add).then_inc(s_rz, 1)
                dve.wait_ge(s_rz, 1)
                dve.reciprocal(rz[:, :, :], rz[:, :, :]).then_inc(s_rz, 3)
                dve.wait_ge(s_rz, 4)

                def h_of(t, j, i):
                    if there(t):
                        h = row(t).rearrange("p (h d) -> p h d", d=D_HEAD)
                        r = rz[:, bass.ds(t, 1), :].rearrange("p a h -> p (a h)").unsqueeze(2).broadcast_to(
                            [P, HEADS, D_HEAD])
                        dve.tensor_tensor(h, h, r, ALU.mult).then_inc(s_h, 1)
                    if j % 2 and there(t - 1):
                        dve.wait_ge(s_h, t)
                        dve.wait_ge(s_ld[j - 1], 16 * (i + 1))
                        dve.tensor_tensor(row(t - 1), row(t - 1), x_sb[:, j - 1, :], ALU.add).then_inc(s_hd, 1)
                tiles(dve, h_of, 0, 1)
                dve.wait_ge(s_mean, 1)

                def centre(t, j, i):
                    dve.tensor_tensor(row(t), row(t), mean[:, :], ALU.subtract).then_inc(s_d, 1)
                tiles(dve, centre)
                dve.wait_ge(s_amp, 1)
                dve.reciprocal(amp[:, :], amp[:, :]).then_inc(s_amp, 1)
                dve.wait_ge(s_amp, 2)
                dve.wait_ge(s_par, 32)
                dve.tensor_tensor(amp[:, :], amp[:, :], gam[:, :], ALU.mult).then_inc(s_amp, 1)
                dve.wait_ge(s_amp, 3)

                def line(t, j, i):
                    a, b, c = j % DEPTH, (j - 1) % DEPTH, (j - 2) % DEPTH
                    if there(t):
                        wait(dve, s_o, t - DEPTH + 1)
                        dve.tensor_tensor(y[:, a, :], row(t), amp[:, :], ALU.mult).then_inc(s_y, 1)
                    if there(t - 2):
                        dve.wait_ge(s_std, t - 1)
                        dve.reciprocal(rstd[:, c, :], std[:, c, :]).then_inc(s_rs, 1)
                    if there(t - 1):
                        dve.wait_ge(s_yx, t)
                        dve.bn_stats(stats[:, b, :], y[:, b, :]).then_inc(s_st, 1)
                    if there(t - 2):
                        dve.wait_ge(s_rs, t - 1)
                        dve.scalar_tensor_tensor(out=shift[:, c, :], in0=mv[:, c, 0:1], scalar=-1.0,
                                                 in1=rstd[:, c, :], op0=ALU.mult, op1=ALU.mult).then_inc(s_sh, 1)
                    if there(t):
                        dve.wait_ge(s_y, t + 1)
                        dve.wait_ge(s_xb, t + 1)
                        dve.tensor_tensor(y[:, a, :], y[:, a, :], sq[:, a, :], ALU.add).then_inc(s_yx, 1)
                    if there(t - 1):
                        wait_apart(dve, s_st, t)
                        dve.bn_aggr(mv[:, b, :], stats[:, b, :]).then_inc(s_mv, 1)
                tiles(dve, line, 1, 2)


def program(nc, xT, x, wq, wk, wv, gamma, beta, edges, dlast, out):
    kv_d = nc.dram_tensor("kv_d", (ROWS, 2 * DIM), F32, kind="Internal").ap()
    q_d = nc.dram_tensor("q_d", (ROWS, 2 * DIM), F32, kind="Internal").ap()
    t_d = nc.dram_tensor("t_d", (VCOLS,), I32, kind="Internal").ap()
    cnt_d = nc.dram_tensor("cnt_d", (64,), I32, kind="Internal").ap()
    with ExitStack() as ctx:
        def sb(name, shape, dt):
            return ctx.enter_context(nc.sbuf_tensor(name, shape, dt))

        tabs = (sb("src_t", [P, VCOLS], I32),
                sb("loc_t", [P, VCOLS], F32),
                sb("bits_row", [1, MASKS], I32),
                sb("cnt_row", [1, 64], I32),
                sb("iota_row", [P, P], F32),
                sb("ident", [P, P], F32))
        project(nc, xT, wq, wk, wv, edges, dlast, kv_d, q_d, t_d, cnt_d, tabs)
        agg = sb("agg", [P, TILES, AGG], F32)
        attend(nc, kv_d, q_d, tabs, agg)
        normalise(nc, x, gamma, beta, out, agg)


def kernel(**inputs):
    import numpy as np
    import concourse.bacc as bacc
    from concourse.bass_utils import run_bass_kernel_spmd

    x = np.zeros((ROWS, DIM), np.float32)
    x[:N_NODES] = inputs["x"]
    edges = np.zeros((BLOCKS_IN * P, 2), np.int32)
    edges[:N_EDGES, 0] = inputs["src"]
    edges[:N_EDGES, 1] = inputs["dst"]
    edges[N_EDGES:BLOCKS * P, 1] = ROWS - 1
    edges[BLOCKS * P:, 1] = -1
    arrays = {
        "xT": np.ascontiguousarray(x.reshape(TILES, P, CHUNKS, P).transpose(0, 3, 2, 1)),
        "x": x,
        "wq": np.ascontiguousarray(inputs["L0_gnn_Wq"]),
        "wk": np.ascontiguousarray(inputs["L0_gnn_Wk"]),
        "wv": np.ascontiguousarray(inputs["L0_gnn_Wv"]),
        "gamma": np.ascontiguousarray(inputs["L0_gnn_bn_gamma"]).reshape(1, DIM),
        "beta": np.ascontiguousarray(inputs["L0_gnn_bn_beta"]).reshape(1, DIM),
        "edges": np.ascontiguousarray(edges.reshape(BLOCKS_IN, P, 2).transpose(0, 2, 1)).reshape(BLOCKS_IN, 2 * P),
        "dlast": np.ascontiguousarray(edges[P - 1::P, 1]).reshape(1, BLOCKS_IN),
    }
    nc = bacc.Bacc("TRN2", target_bir_lowering=False, num_devices=1)
    aps = {}
    for name, a in arrays.items():
        aps[name] = nc.dram_tensor(f"in_{name}", a.shape, mybir.dt.from_np(a.dtype), kind="ExternalInput").ap()
    out = nc.dram_tensor("out_rows", (ROWS, DIM), F32, kind="ExternalOutput").ap()
    program(nc, out=out, **aps)
    got = run_bass_kernel_spmd(nc, [{f"in_{n}": a for n, a in arrays.items()}], core_ids=[0])
    return got.results[0]["out_rows"][:N_NODES]
```

```python
from contextlib import ExitStack

import concourse.bass as bass
from concourse import mybir

F32 = mybir.dt.float32
BF16 = mybir.dt.bfloat16
I32 = mybir.dt.int32
F32R = mybir.dt.float32r
U32 = mybir.dt.uint32
ALU = mybir.AluOpType
ACT = mybir.ActivationFunctionType
AX = mybir.AxisListType

P = 128
N_NODES, DIM, HEADS = 6250, 512, 8
D_HEAD = DIM // HEADS
N_EDGES = 106250
TILES = -(-N_NODES // P)
ROWS = TILES * P
BLOCKS = -(-N_EDGES // P)
BLOCKS_IN = BLOCKS + 1
STAIRS = BLOCKS + TILES - 1
PAIRS = -(-STAIRS // 2)
VISITS = 2 * PAIRS
VTILES = -(-(VISITS + 1) // P)
VCOLS = VTILES * P
RING = 9
ROUNDS = PAIRS // RING
IDX_PAIRS = 3
MT_RING = 3
Q_BANKS = 3
CHUNKS = DIM // P
SKIP = 65536.0
SLOTS = 8
DEPTH = 4
ACT_HEADS = 5
POOL_HEADS = 2
AGG = DIM + 2 * HEADS
VBODY = 2 * RING
MASKS = -(-(VISITS + VBODY - 2) // VBODY)
LAST_ROWS = N_NODES - (TILES - 1) * P


def wait(eng, sem, value):
    if not (isinstance(value, int) and value <= 0):
        eng.wait_ge(sem, value)


def wait_apart(eng, sem, value):
    if not isinstance(value, int):
        value = eng.snap(eng.to_reg(value))
        eng.wait_ge(sem, 1)
    wait(eng, sem, value)


def project(nc, xT, wq, wk, wv, edges, dlast, kv_d, q_d, t_d, cnt_d, tabs):
    src_t, loc_t, bits_row, cnt_row, iota_row, ident = tabs
    with ExitStack() as ctx:
        def sb(name, shape, dt):
            return ctx.enter_context(nc.sbuf_tensor(name, shape, dt))

        def sem(name):
            return ctx.enter_context(nc.semaphore(name))

        w_sb = sb("w_sb", [P, 3, CHUNKS, DIM], F32)
        x_sb = [sb(f"x_sb{j}", [P, CHUNKS, P], F32) for j in range(2)]
        kv_sb = [sb(f"kv_sb{j}", [P, 2 * DIM], F32) for j in range(2)]
        q_sb = [sb(f"q_sb{j}", [P, 2, DIM], F32) for j in range(2)]
        kv_ps = [ctx.enter_context(nc.psum_tensor(f"kv_ps{j}", [P, 2 * DIM], F32)) for j in range(2)]
        q_ps = [ctx.enter_context(nc.psum_tensor(f"q_ps{j}", [P, DIM], F32)) for j in range(2)]
        tab_ps = ctx.enter_context(nc.psum_tensor("tab_ps", [P, 2, 512], F32))
        dl = sb("dl", [P, BLOCKS_IN], I32)
        k128 = sb("k128", [P, BLOCKS_IN], I32)
        ends = sb("ends", [P, BLOCKS_IN], F32)
        below = sb("below", [P, VCOLS], F32)
        v128i = sb("v128i", [P, VTILES], I32)
        v128 = sb("v128", [P, VTILES], F32)
        kf = sb("kf", [P, VTILES], F32)
        ki = sb("ki", [P, VTILES], I32)
        t128 = sb("t128", [P, VTILES], F32)
        ti = sb("ti", [P, VTILES], I32)
        rows = sb("rows", [P, VTILES, 2 * P], I32)
        loc = sb("loc", [P, VCOLS], F32)
        srcf = sb("srcf", [P, VCOLS], F32)
        skip = sb("skip", [P, VCOLS], F32)
        iota_i = sb("iota_i", [P, P], I32)
        col_i = sb("col_i", [P, 1], I32)
        col = sb("col", [P, 1], F32)
        t_bc = sb("t_bc", [64, VCOLS], I32)
        t_row = sb("t_row", [1, VCOLS], I32)
        steps = sb("steps", [1, MASKS * VBODY], F32)
        powers = sb("powers", [1, VBODY], F32)
        masks = sb("masks", [1, MASKS], F32)
        cnt = sb("cnt", [64, 1], F32)
        cnti = sb("cnti", [64, 1], I32)

        s_wq = [sem(f"s_wq{c}") for c in range(CHUNKS)]
        s_wkv = [sem("s_wk"), sem("s_wv")]
        s_x = [sem(f"s_x{j}") for j in range(2)]
        s_kvst = [sem(f"s_kvst{j}") for j in range(2)]
        s_qst = [sem(f"s_qst{j}") for j in range(2)]
        s_proj, s_kvc = sem("s_proj"), sem("s_kvc")
        s_qh, s_ql = sem("s_qh"), sem("s_ql")
        s_dl, s_iota, s_tab, s_rows = sem("s_dl"), sem("s_iota"), sem("s_tab"), sem("s_rows")
        s_visit, s_tr, s_trc, s_td, s_tb, s_cnt = (sem("s_visit"), sem("s_tr"), sem("s_trc"), sem("s_td"),
                                                   sem("s_tb"), sem("s_cnt"))
        cuts = [0, 8, 16, (TILES - 1) // 2]

        def tiles(eng, part, step):
            with eng.Fori(cuts[part], cuts[part + 1]) as i:
                for j in range(2):
                    step(i, j)

        with nc.Block() as block:
            @block.sync
            def _(sp):
                sp.dma_start(x_sb[0][:, :, :], xT[0]).then_inc(s_x[0], 16)
                for c in range(CHUNKS):
                    sp.dma_start(w_sb[:, 0, c, :], wq[c * P:(c + 1) * P, :]).then_inc(s_wq[c], 16)
                for n, w in ((1, wk), (2, wv)):
                    sp.dma_start(w_sb[:, n, :, :], w.rearrange("(c p) n -> p c n", p=P)).then_inc(s_wkv[n - 1], 16)
                sp.dma_start(x_sb[1][:, :, :], xT[1]).then_inc(s_x[1], 16)

                def step(i, j, more=True):
                    tile = 2 * i + j
                    if more:
                        sp.wait_ge(s_proj, tile + 1)
                        sp.dma_start(x_sb[j][:, :, :], xT[bass.ds(tile + 2, 1)].rearrange("a p c n -> (a p) c n")
                                     if not isinstance(tile, int) else xT[tile + 2]).then_inc(s_x[j], 16)
                    sp.wait_ge(s_ql, tile + 1)
                    sp.dma_start(q_d[bass.ds(tile * P, P), :],
                                 q_sb[j][:, :, :].rearrange("p a n -> p (a n)")).then_inc(s_qst[j], 16)
                with sp.Fori(0, cuts[3] - 1) as i:
                    for j in range(2):
                        step(i, j)
                step(cuts[3] - 1, 0)
                step(cuts[3] - 1, 1, False)
                step(cuts[3], 0, False)
                for j in range(2):
                    sp.wait_ge(s_qst[j], 16 * (cuts[3] + 1 - j))
                    sp.wait_ge(s_kvst[j], 16 * (cuts[3] + 1 - j))

            @block.gpsimd
            def _(pool):
                pool.dma_start(dl[:, :], dlast.broadcast_to([P, BLOCKS_IN])).then_inc(s_dl, 16)
                pool.iota(k128[:, :], pattern=[[P, BLOCKS_IN]], base=0, channel_multiplier=0)
                pool.iota(v128i[:, :], pattern=[[P * P, VTILES]], base=0, channel_multiplier=P)
                pool.iota(col_i[:, :], pattern=[[1, 1]], base=0, channel_multiplier=1)
                pool.iota(iota_i[:, :], pattern=[[1, P]], base=0, channel_multiplier=0).then_inc(s_iota, 1)
                pool.wait_ge(s_visit, 1)
                for a in range(VTILES):
                    pool.indirect_dma_start(rows[:, a, :], None, edges,
                                            bass.IndirectOffsetOnAxis(ki[:, a:a + 1], 0),
                                            bounds_check=BLOCKS_IN - 1, oob_is_err=False).then_inc(s_rows, 16)
                pool.dma_start(t_d.rearrange("(a p) -> p a", p=P), ti[:, :],
                               allow_slow_non_contiguous=True).then_inc(s_td, 16)
                pool.wait_ge(s_td, 16)
                pool.dma_start(t_row[:, :], t_d.rearrange("(a n) -> a n", a=1)).then_inc(s_tb, 16)
                pool.dma_start(t_bc[:, :], t_d.rearrange("(a n) -> a n", a=1).broadcast_to([64, VCOLS])
                               ).then_inc(s_tb, 16)
                pool.wait_ge(s_cnt, 3)
                pool.dma_start(cnt_d.rearrange("(p a) -> p a", a=1), cnti[:, :],
                               allow_slow_non_contiguous=True).then_inc(s_td, 16)
                pool.wait_ge(s_td, 32)
                pool.dma_start(cnt_row[:, :], cnt_d.rearrange("(a n) -> a n", a=1)).then_inc(s_tb, 16)
                pool.wait_ge(s_tb, 48)

            @block.tensor
            def _(pe):
                def step(i, j, first=False):
                    tile = 2 * i + j
                    pe.wait_ge(s_x[j], 16 * (i + 1))
                    wait(pe, s_kvc, tile - 1)
                    wait(pe, s_ql, tile - 1)
                    for n, out in enumerate((q_ps[j][:, :], kv_ps[j][:, 0:DIM], kv_ps[j][:, DIM:2 * DIM])):
                        if first and n:
                            pe.wait_ge(s_wkv[n - 1], 16)
                        for c in range(CHUNKS):
                            if first and n == 0:
                                pe.wait_ge(s_wq[c], 16)
                            last = pe.matmul(out, x_sb[j][:, c, :], w_sb[:, n, c, :],
                                             start=(c == 0), stop=(c == CHUNKS - 1))
                    last.then_inc(s_proj, 1)
                for j in range(2):
                    step(0, j, j == 0)
                with pe.Fori(1, cuts[1]) as i:
                    for j in range(2):
                        step(i, j)
                tiles(pe, 1, step)
                pe.wait_ge(s_visit, 3)
                for n, tab in enumerate((srcf, loc)):
                    if n:
                        pe.wait_ge(s_trc, 1)
                    for a in range(VTILES):
                        last = pe.transpose(tab_ps[:, a // 4, (a % 4) * P:(a % 4 + 1) * P],
                                            tab[:, a * P:(a + 1) * P], ident[:, :])
                    last.then_inc(s_tr, 1)
                tiles(pe, 2, step)
                step(cuts[3], 0)

            @block.scalar
            def _(act):
                def step(i, j):
                    tile = 2 * i + j
                    act.wait_ge(s_proj, tile + 1)
                    wait(act, s_kvst[j], 16 * i)
                    act.copy(kv_sb[j][:, :], kv_ps[j][:, :]).then_inc(s_kvc, 1)
                    act.wait_ge(s_kvc, tile + 1)
                    act.dma_start(kv_d[bass.ds(tile * P, P), :], kv_sb[j][:, :]).then_inc(s_kvst[j], 16)
                for j in range(2):
                    step(0, j)
                with act.Fori(1, cuts[3]) as i:
                    for j in range(2):
                        step(i, j)
                step(cuts[3], 0)

            @block.vector
            def _(dve):
                n_tab = [0]

                def tab(ins):
                    ins.then_inc(s_tab, 1)
                    n_tab[0] += 1
                    dve.wait_ge(s_tab, n_tab[0])

                dve.wait_ge(s_iota, 1)
                dve.wait_ge(s_dl, 16)
                tab(dve.tensor_copy(iota_row[:, :], iota_i[:, :]))
                tab(dve.tensor_copy(col[:, :], col_i[:, :]))
                tab(dve.tensor_scalar(ident[:, :], iota_row[:, :], col[:, 0:1], None, ALU.is_equal))
                tab(dve.tensor_copy(v128[:, :], v128i[:, :]))
                tab(dve.tensor_tensor(ends[:, :], dl[:, :], k128[:, :], ALU.add))
                for a in range(VTILES):
                    tab(dve.tensor_scalar(below[:, 0:BLOCKS], ends[:, 0:BLOCKS], v128[:, a:a + 1], None,
                                          ALU.is_lt))
                    tab(dve.tensor_reduce(kf[:, a:a + 1], below[:, 0:BLOCKS], AX.X, ALU.add))
                tab(dve.tensor_copy(ki[:, :], kf[:, :]))
                tab(dve.tensor_scalar(kf[:, :], kf[:, :], float(P), None, ALU.mult))
                tab(dve.tensor_tensor(t128[:, :], v128[:, :], kf[:, :], ALU.subtract))
                dve.tensor_scalar(ti[:, :], t128[:, :], 1.0 / P, None, ALU.mult).then_inc(s_visit, 1)

                def step(i, j):
                    tile = 2 * i + j
                    dve.wait_ge(s_proj, tile + 1)
                    wait(dve, s_qst[j], 16 * i)
                    hi, lo = (q_sb[j][:, n, :] for n in range(2))
                    dve.tensor_scalar(hi.bitcast(F32R), q_ps[j][:, :], D_HEAD ** -0.5, None,
                                      ALU.mult).then_inc(s_qh, 1)
                    dve.wait_ge(s_qh, tile + 1)
                    dve.scalar_tensor_tensor(out=lo.bitcast(F32R), in0=q_ps[j][:, :], scalar=D_HEAD ** -0.5,
                                             in1=hi, op0=ALU.mult, op1=ALU.subtract).then_inc(s_ql, 1)
                for j in range(2):
                    step(0, j)
                with dve.Fori(1, cuts[1]) as i:
                    for j in range(2):
                        step(i, j)
                dve.wait_ge(s_rows, 16 * VTILES)
                for a in range(VTILES):
                    last = dve.tensor_scalar(loc[:, a * P:(a + 1) * P], rows[:, a, P:2 * P],
                                             t128[:, a:a + 1], None, ALU.subtract)
                tab(last)
                tab(dve.tensor_scalar(skip[:, :], loc[:, :], 0.0, SKIP, ALU.is_lt, ALU.mult))
                tab(dve.tensor_tensor(srcf[:, :].rearrange("p (a n) -> p a n", n=P), rows[:, :, 0:P],
                                      skip[:, :].rearrange("p (a n) -> p a n", n=P), ALU.add))
                tab(dve.tensor_scalar(skip[:, :], loc[:, :], float(P - 1), SKIP, ALU.is_gt, ALU.mult))
                tab(dve.tensor_tensor(srcf[:, :], srcf[:, :], skip[:, :], ALU.add))
                dve.tensor_copy(srcf[0:2 * RING, 0:P], rows[0:2 * RING, 0, 0:P]).then_inc(s_visit, 2)
                tab(dve.memset(powers[:, :], 1.0))
                tab(dve.memset(steps[:, :], 0.0))
                dve.wait_ge(s_tb, 32)
                n = 1
                while n < VBODY:
                    m = min(n, VBODY - n)
                    tab(dve.tensor_scalar(powers[:, n:n + m], powers[:, 0:m], float(2 ** n), None, ALU.mult))
                    n += m
                last_v = MASKS * VBODY - (VBODY - 2) - 1
                last_v = min(last_v, VISITS)
                tab(dve.tensor_tensor(steps[:, VBODY - 1:VBODY - 1 + last_v], t_row[:, 1:last_v + 1],
                                      t_row[:, 0:last_v], ALU.subtract))
                by_mask = steps[:, :].rearrange("p (m k) -> p m k", k=VBODY)
                tab(dve.tensor_tensor(by_mask, by_mask, powers[:, :].unsqueeze(1).broadcast_to([1, MASKS, VBODY]),
                                      ALU.mult))
                tab(dve.tensor_reduce(masks[:, :], by_mask, AX.X, ALU.add))
                tab(dve.tensor_copy(bits_row[:, :], masks[:, :]))
                dve.tensor_scalar(below[0:64, :], t_bc[:, :], col[0:64, 0:1], None,
                                  ALU.is_le).then_inc(s_cnt, 1)
                dve.wait_ge(s_cnt, 1)
                dve.tensor_reduce(cnt[:, :], below[0:64, :], AX.X, ALU.add).then_inc(s_cnt, 1)
                dve.wait_ge(s_cnt, 2)
                dve.tensor_copy(cnti[:, :], cnt[:, :]).then_inc(s_cnt, 1)
                tiles(dve, 1, step)
                half = tab_ps[:, :, :].rearrange("p a n -> p (a n)")[:, 0:VCOLS]
                dve.wait_ge(s_tr, 1)
                dve.tensor_copy(src_t[:, :], half).then_inc(s_trc, 1)
                dve.wait_ge(s_tr, 2)
                dve.tensor_copy(loc_t[:, :], half).then_inc(s_trc, 1)
                tiles(dve, 2, step)
                step(cuts[3], 0)


def attend(nc, kv_d, q_d, tabs, agg):
    src_t, loc_t, bits_row, cnt_row, iota_row, ident = tabs
    with ExitStack() as ctx:
        def sb(name, shape, dt):
            return ctx.enter_context(nc.sbuf_tensor(name, shape, dt))

        def ps(name, shape, dt):
            return ctx.enter_context(nc.psum_tensor(name, shape, dt))

        def sem(name):
            return ctx.enter_context(nc.semaphore(name))

        kv = sb("kv", [P, RING, 2, 2 * DIM], F32)
        idx = sb("idx", [P, RING, 2], I32)
        q_tile = sb("q_tile", [P, 2, 2 * DIM], F32)
        m_sb = sb("m_sb", [P, RING, 2, P], F32)
        mt_sb = sb("mt_sb", [P, MT_RING, 2 * P], F32R)
        raw = sb("raw", [P, RING, 2, HEADS], F32)
        score = sb("score", [P, RING, 2, HEADS], F32)
        zeros = sb("zeros", [P, DIM], BF16)
        idle = sb("idle", [P, 1], F32)
        acc = ps("acc", [P, 2, DIM], F32)
        parts = sb("parts", [P, RING, 2, 2 * HEADS], F32R)
        z_acc = ps("z_acc", [P, 2, DIM], F32)
        t_ps = ps("t_ps", [P, 8 * P], BF16)
        q_ps = ps("q_ps", [P, Q_BANKS, DIM], F32)

        s_g = [[sem(f"s_g{s}_{u}") for u in range(2)] for s in range(RING)]
        s_idx, s_m, s_t, s_mt, s_qx = sem("s_idx"), sem("s_m"), sem("s_t"), sem("s_mt"), sem("s_qx")
        s_mul, s_red, s_clip, s_exp, s_va, s_vd = (sem("s_mul"), sem("s_red"), sem("s_clip"), sem("s_exp"),
                                                   sem("s_va"), sem("s_vd"))
        s_seg, s_evc, s_evict, s_q = sem("s_seg"), sem("s_evc"), sem("s_evict"), sem("s_q")
        s_split, s_part = sem("s_split"), sem("s_part")
        SPLIT_LAG = 6
        LOOKAHEAD, LAG = 3, 3

        def pipeline(eng, step):
            for q in range(-LOOKAHEAD, RING):
                step(q, q % RING, 1)
            with eng.Fori(1, ROUNDS - 1) as i:
                for s in range(RING):
                    step(i * RING + s, s, i + 1)
            for q in range((ROUNDS - 1) * RING, PAIRS + LAG):
                step(q, q % RING, q // RING + 1)

        def there(q):
            return not isinstance(q, int) or 0 <= q < PAIRS

        def follow(eng, tiles):
            now, before = eng.alloc_register("mask_now"), eng.alloc_register("mask_before")
            regs = [eng.alloc_register(f"tile_{n}") for n in range(tiles)]
            for r in (now, *regs):
                eng.reg_mov(r, 0)

            def fetch(mask):
                eng.reg_mov(before, now)
                if not isinstance(mask, int) or mask < MASKS:
                    eng.reg_load(now, bits_row[0:1, bass.ds(mask, 1)])

            def bit(k, earlier=False):
                mask = eng.snap(before if earlier else now, min_val=0, max_val=2 ** VBODY - 1)
                return (mask >> k) & 1
            fetch(0)
            return regs, fetch, bit

        def as_bf16(ap):
            return ap.bitcast(BF16).rearrange("p (n h) -> p n h", h=2)[:, :, 1]

        def part(s, n):
            return parts[:, s, :, n * HEADS:(n + 1) * HEADS]

        def heads(ap):
            return ap.rearrange("p a (h d) -> p a h d", d=D_HEAD)

        with nc.Block() as block:
            @block.sync
            def _(sp):
                def load(t):
                    sp.dma_start(q_tile[:, bass.ds(t % 2, 1), :].rearrange("p a n -> p (a n)"),
                                 q_d[bass.ds(t * P, P), :]).then_inc(s_q, 16)
                load(0)
                sp.wait_ge(s_q, 16)
                load(1)
                with sp.Fori(2, TILES) as t:
                    used = sp.value_load(cnt_row[0:1, bass.ds(t - 2, 1)], min_val=1, max_val=VISITS)
                    wait_apart(sp, s_qx, used)
                    sp.wait_ge(s_q, 16 * t)
                    load(t)

            @block.gpsimd
            def _(pool):
                def index(q, s, fills):
                    last = s + IDX_PAIRS - 1
                    wait(pool, s_g[last][1], 16 * (fills - 1))
                    pool.tensor_copy(idx[:, s:last + 1, :].rearrange("p a n -> p (a n)"),
                                     src_t[:, bass.ds(2 * q, 2 * IDX_PAIRS)]).then_inc(s_idx, 1)

                def gather(q, s, fills, u):
                    if u == 0 and s % IDX_PAIRS == 0:
                        wait_apart(pool, s_idx, (fills - 1) * (RING // IDX_PAIRS) + s // IDX_PAIRS + 1)
                    if u == 0:
                        wait_apart(pool, s_seg, q - RING + 1)
                    pool.indirect_dma_start(kv[:, s, u, :], None, kv_d,
                                            bass.IndirectOffsetOnAxis(idx[:, s, u:u + 1], 0),
                                            bounds_check=N_NODES - 1, oob_is_err=False
                                            ).then_inc(s_g[s][u], 16)

                def split_hi(p, s):
                    if there(p):
                        wait_apart(pool, s_exp, p + 1)
                        pool.tensor_copy(part(s, 0), score[:, s, :, :]).then_inc(s_split, 1)

                def split_lo(p, s):
                    if there(p):
                        wait_apart(pool, s_split, p + 1)
                        pool.tensor_tensor(part(s, 1), score[:, s, :, :], part(s, 0).bitcast(F32),
                                           ALU.subtract).then_inc(s_part, 1)

                def messages(p, s):
                    if there(p):
                        v = heads(kv[:, s, :, DIM:2 * DIM])[:, :, ACT_HEADS:ACT_HEADS + POOL_HEADS, :]
                        w = score[:, s, :, ACT_HEADS:ACT_HEADS + POOL_HEADS].unsqueeze(3).broadcast_to(
                            [P, 2, POOL_HEADS, D_HEAD])
                        wait_apart(pool, s_va, p + 1)
                        wait_apart(pool, s_vd, p + 2)
                        pool.tensor_tensor(v, v, w, ALU.mult).then_inc(s_part, 1)

                def step(q, s, fills):
                    p, sp = q - SPLIT_LAG, (s - SPLIT_LAG) % RING
                    if there(q) and s % IDX_PAIRS == 0:
                        index(q, s, fills)
                    split_hi(p, sp)
                    if there(q):
                        gather(q, s, fills, 0)
                    split_lo(p, sp)
                    if there(q):
                        gather(q, s, fills, 1)
                    messages(p, sp)
                for s in range(RING):
                    step(s, s, 1)
                with pool.Fori(1, ROUNDS) as i:
                    for s in range(RING):
                        step(i * RING + s, s, i + 1)
                for q in range(ROUNDS * RING, PAIRS + SPLIT_LAG):
                    step(q, q % RING, q // RING + 1)

            @block.vector
            def _(dve):
                dve.memset(zeros[:, :], 0.0).then_inc(s_vd, 1)

                def step(q, s, fills):
                    a = q + LOOKAHEAD
                    sa, s1 = (s + LOOKAHEAD) % RING, (s - 1) % RING
                    if there(q):
                        for u in range(2):
                            dve.wait_ge(s_g[s][u], 16 * fills)
                            dve.wait_ge(s_qx, 2 * q + u + 1)
                            k = kv[:, s, u, 0:DIM]
                            dve.tensor_tensor(k, q_ps[:, (2 * s + u) % Q_BANKS, :], k, ALU.mult).then_inc(s_mul, 1)
                    if there(a):
                        wait(dve, s_seg, a - RING + 1)
                        dve.tensor_tensor(m_sb[:, sa, :, :].bitcast(F32R),
                                          iota_row[:, :].unsqueeze(1).broadcast_to([P, 2, P]),
                                          loc_t[:, bass.ds(2 * a, 2)].unsqueeze(2).broadcast_to([P, 2, P]),
                                          ALU.is_equal).then_inc(s_m, 1)
                    if there(q):
                        dve.wait_ge(s_mul, 2 * q + 2)
                        dve.tensor_reduce(raw[:, s, :, :], heads(kv[:, s, :, 0:DIM]), AX.X,
                                          ALU.add).then_inc(s_red, 1)
                    if there(q - 1):
                        dve.wait_ge(s_exp, q)
                        v = heads(kv[:, s1, :, DIM:2 * DIM])[:, :, ACT_HEADS + POOL_HEADS:, :]
                        w = score[:, s1, :, ACT_HEADS + POOL_HEADS:].unsqueeze(3).broadcast_to(
                            [P, 2, HEADS - ACT_HEADS - POOL_HEADS, D_HEAD])
                        dve.tensor_tensor(v, v, w, ALU.mult).then_inc(s_vd, 1)
                    if there(q):
                        dve.wait_ge(s_red, q + 1)
                        dve.tensor_scalar(raw[:, s, :, :], raw[:, s, :, :], -5.0, 5.0, ALU.max,
                                          ALU.min).then_inc(s_clip, 1)

                pipeline(dve, step)

            @block.scalar
            def _(act):
                act.memzero(idle[:, :]).then_inc(s_evict, 2)

                (tile_reg,), fetch, bit = follow(act, 1)

                def evict(t):
                    par = t % 2
                    act.copy(agg[:, bass.ds(t, 1), 0:DIM], acc[:, bass.ds(par, 1), :])
                    act.copy(agg[:, bass.ds(t, 1), DIM:AGG],
                             z_acc[:, bass.ds(par, 1), 0:2 * HEADS]).then_inc(s_evc, 1)
                    wait_apart(act, s_evc, t + 1)
                    act.mul(acc[:, bass.ds(par, 1), :].bitcast(U32), acc[:, bass.ds(par, 1), :].bitcast(U32), 0.0)
                    z = z_acc[:, bass.ds(par, 1), 0:2 * HEADS].bitcast(U32)
                    act.mul(z, z, 0.0).then_inc(s_evict, 1)

                def step(q, s, fills):
                    e, a = q - LAG, q + 2
                    sa = (s + 2) % RING
                    if there(e):
                        t0 = act.snap(tile_reg, min_val=0, max_val=TILES - 1)
                        over = act.snap(sum(bit((2 * (s - LAG) + n + VBODY - 2) % VBODY,
                                                earlier=2 * (s - LAG) + n + VBODY - 2 < VBODY) for n in (1, 2)),
                                        min_val=0, max_val=2)
                        with act.If(over > 0):
                            act.wait_ge(s_seg, e + 1)
                            evict(t0)
                            with act.If(over > 1):
                                evict((t0 + 1).with_bounds(min_val=1, max_val=TILES - 1))
                        act.reg_mov(tile_reg, t0 + over)
                    if there(a):
                        act.wait_ge(s_t, a + 1)
                        act.copy(mt_sb[:, sa % MT_RING, :], t_ps[:, 0:2 * P]).then_inc(s_mt, 1)
                    if there(q):
                        act.wait_ge(s_clip, q + 1)
                        act.activation(score[:, s, :, :], raw[:, s, :, :], ACT.Exp).then_inc(s_exp, 1)
                        act.wait_ge(s_exp, q + 1)
                        for u in range(2):
                            for h in range(ACT_HEADS):
                                v = kv[:, s, u, DIM + h * D_HEAD:DIM + (h + 1) * D_HEAD]
                                last = act.activation(v, v, ACT.Copy, scale=score[:, s, u, h:h + 1])
                        last.then_inc(s_va, 1)
                    if s == RING - 1:
                        fetch(q // RING + 2 if isinstance(q, int) else fills + 1)
                pipeline(act, step)

            @block.tensor
            def _(pe):
                PLACES = RING
                tile_regs, fetch, bit = follow(pe, PLACES)
                pe.wait_ge(s_vd, 1)
                for par in range(2):
                    pe.matmul(acc[:, par, :], zeros[:, 0:P], zeros[:, :], start=True, stop=True)
                    pe.matmul(z_acc[:, par, 0:2 * HEADS], zeros[:, 0:P], zeros[:, 0:2 * HEADS], start=True,
                              stop=True)

                def step(q, s, fills):
                    a, b, c = q + 3, q + 1, q - 2
                    sa, sb_, sc = (s + 3) % RING, (s + 1) % RING, (s - 2) % RING
                    if there(b):
                        for u in range(2):
                            v = 2 * sb_ + u
                            tile = pe.snap(pe.snap(tile_regs[(v - 1) % PLACES], min_val=0, max_val=TILES - 1)
                                           + bit(2 * s + u), min_val=0, max_val=TILES - 1)
                            pe.reg_mov(tile_regs[v % PLACES], tile)
                            if u == 0:
                                pe.wait_ge(s_mt, b + 1)
                            wait(pe, s_mul, 2 * b + u + 1 - Q_BANKS)
                            pe.wait_ge(s_q, 16 * (tile + 1))
                            for n in range(2):
                                part_q = q_tile[:, bass.ds(tile % 2, 1), n * DIM:(n + 1) * DIM].bitcast(F32R)
                                last = pe.matmul(q_ps[:, (2 * sb_ + u) % Q_BANKS, :],
                                                 mt_sb[:, sb_ % MT_RING, u * P:(u + 1) * P], part_q,
                                                 start=(n == 0), stop=(n == 1))
                            last.then_inc(s_qx, 1)
                    if there(c):
                        wait_apart(pe, s_part, 2 * (c + 1))
                        banks = []

                        def z_sum(u):
                            return pe.matmul(z_acc[:, banks[u], 0:2 * HEADS], m_sb[:, sc, u, :].bitcast(F32R),
                                             parts[:, sc, u, :], start=False, stop=True, skip_group_check=True)
                        for u in range(2):
                            tile = pe.snap(tile_regs[(2 * sc + u) % PLACES], min_val=0, max_val=TILES - 1)
                            pe.wait_ge(s_evict, tile + 1)
                            banks.append(bass.ds(tile % 2, 1))
                            if u == 0:
                                z_sum(0)
                            pe.matmul(acc[:, banks[u], :], m_sb[:, sc, u, :],
                                      kv[:, sc, u, DIM:2 * DIM], start=False, stop=True, skip_group_check=True)
                        last = z_sum(1)
                        last.then_inc(s_seg, 1)
                    if s == RING - 1:
                        fetch(q // RING + 2 if isinstance(q, int) else fills + 1)
                    if there(a):
                        pe.wait_ge(s_m, a + 1)
                        wait(pe, s_mt, a)
                        for u in range(2):
                            last = pe.transpose(t_ps[:, u * P:(u + 1) * P], as_bf16(m_sb[:, sa, u, :]),
                                                as_bf16(ident[:, :]))
                        last.then_inc(s_t, 1)
                pipeline(pe, step)


def normalise(nc, x, gamma, beta, out, ident, agg):
    with ExitStack() as ctx:
        def sb(name, shape, dt):
            return ctx.enter_context(nc.sbuf_tensor(name, shape, dt))

        def sem(name):
            return ctx.enter_context(nc.semaphore(name))

        x_sb = sb("x_res", [P, SLOTS, DIM], F32)
        rz = sb("rz", [P, TILES, HEADS], F32)
        gam, bet = sb("gam", [P, DIM], F32), sb("bet", [P, DIM], F32)
        mean, amp = sb("mean", [P, DIM], F32), sb("amp", [P, DIM], F32)
        ones, ones_last = sb("ones", [P, P], F32), sb("ones_last", [P, P], F32)
        sq = sb("sq", [P, DEPTH, DIM], F32)
        xb = sb("xb", [P, DEPTH, DIM], F32)
        y = sb("y", [P, DEPTH, DIM], F32)
        stats = sb("stats", [P, DEPTH, 6], F32)
        mv = sb("mv", [P, DEPTH, 2], F32)
        std, rstd, shift = (sb(name, [P, DEPTH, 1], F32) for name in ("std", "rstd", "shift"))
        o_sb = sb("o_sb", [P, DEPTH, DIM], F32)
        eps = sb("eps", [P, 1], F32)
        sum_ps = ctx.enter_context(nc.psum_tensor("sum_ps", [P, DIM], F32))
        var_ps = ctx.enter_context(nc.psum_tensor("var_ps", [P, DIM], F32))
        y_ps = ctx.enter_context(nc.psum_tensor("y_ps", [P, DEPTH, DIM], F32))

        s_ld, s_par, s_one = [sem(f"s_ld{j}") for j in range(SLOTS)], sem("s_par"), sem("s_one")
        s_rz, s_h, s_hx, s_hd, s_sum = sem("s_rz"), sem("s_h"), sem("s_hx"), sem("s_hd"), sem("s_sum")
        s_mean, s_d, s_sq, s_var, s_amp = sem("s_mean"), sem("s_d"), sem("s_sq"), sem("s_var"), sem("s_amp")
        s_xb, s_y, s_yx, s_st, s_mv, s_std = (sem("s_xb"), sem("s_y"), sem("s_yx"), sem("s_st"), sem("s_mv"),
                                              sem("s_std"))
        s_rs, s_sh, s_o = sem("s_rs"), sem("s_sh"), sem("s_o")
        s_out = [sem(f"s_out{j}") for j in range(DEPTH)]
        BODIES = TILES // SLOTS
        assert BODIES * SLOTS == TILES - 1 and SLOTS % DEPTH == 0

        def row(t):
            return agg[:, bass.ds(t, 1), 0:DIM].rearrange("p a n -> p (a n)")

        def tiles(eng, step, ahead=0, behind=0):
            for t in range(ahead * SLOTS):
                step(t, t % SLOTS, t // SLOTS)
            with eng.Fori(ahead, BODIES) as i:
                for j in range(SLOTS):
                    step(i * SLOTS + j, j, i)
            for t in range(BODIES * SLOTS, TILES + behind):
                step(t, t % SLOTS, t // SLOTS)

        def there(t):
            return not isinstance(t, int) or 0 <= t < TILES

        def weights(t):
            return ones_last if isinstance(t, int) and t == TILES - 1 else ones

        with nc.Block() as block:
            @block.sync
            def _(sp):
                sp.dma_start(gam[:, :], gamma.broadcast_to([P, DIM])).then_inc(s_par, 16)
                sp.dma_start(bet[:, :], beta.broadcast_to([P, DIM])).then_inc(s_par, 16)

                def load(t, j, i, used):
                    for sem_used, n in used(t, j):
                        wait_apart(sp, sem_used, n)
                    sp.dma_start(x_sb[:, j, :], x[bass.ds(t * P, P), :]).then_inc(s_ld[j], 16)

                def first(t, j, i):
                    n = (i - 1) * (SLOTS // 2) + j // 2 + 1
                    load(t, j, i, lambda t, j: [(s_hx if j % 2 else s_hd, n)])
                tiles(sp, first, 1)
                sp.wait_ge(s_hd, TILES // 2 + 1)
                sp.wait_ge(s_hx, TILES // 2)

                def second(t, j, i):
                    load(t, j, i, lambda t, j: [(s_xb, t - SLOTS + 1)])
                tiles(sp, second, 1)

            @block.gpsimd
            def _(pool):
                pool.memset(ones[:, :], 1.0)
                pool.memset(ones_last[:, :], 1.0).then_inc(s_one, 1)
                pool.wait_ge(s_one, 1)
                pool.affine_select(out=ones_last[:, :], in_=ones_last[:, :], compare_op=ALU.is_ge, fill=0.0,
                                   base=LAST_ROWS - 1, pattern=[[0, P]], channel_multiplier=-1).then_inc(s_one, 1)

                def add_x(t, j, i):
                    if j % 2:
                        pool.wait_ge(s_ld[j], 16 * (i + 1))
                        pool.wait_ge(s_h, t + 1)
                        pool.tensor_tensor(row(t), row(t), x_sb[:, j, :], ALU.add).then_inc(s_hx, 1)
                tiles(pool, add_x)
                pool.wait_ge(s_par, 32)

                def x_beta(t, j, i):
                    d = j % DEPTH
                    pool.wait_ge(s_ld[j], 16 * (i + 1 + BODIES + (j == 0)))
                    wait(pool, s_yx, t - DEPTH + 1)
                    pool.tensor_tensor(xb[:, d, :], x_sb[:, j, :], bet[:, :], ALU.add).then_inc(s_xb, 1)
                tiles(pool, x_beta, 1)

            @block.tensor
            def _(pe):
                pe.wait_ge(s_one, 2)
                pe.wait_ge(s_rz, 4)
                for ps in (sum_ps, var_ps):
                    pe.matmul(ps[:, :], ones[:, :], sq[:, 0, :], start=True, stop=True).then_inc(s_sum, 1)

                def colsum(t, j, i):
                    pe.wait_ge(s_hx if j % 2 else s_hd, i * (SLOTS // 2) + j // 2 + 1)
                    pe.matmul(sum_ps[:, :], weights(t)[:, :], row(t), start=False, stop=True,
                              skip_group_check=True).then_inc(s_sum, 1)
                tiles(pe, colsum)

                def colsquare(t, j, i):
                    pe.wait_ge(s_sq, t + 1)
                    pe.matmul(var_ps[:, :], weights(t)[:, :], sq[:, j % DEPTH, :], start=False, stop=True,
                              skip_group_check=True).then_inc(s_var, 1)
                tiles(pe, colsquare)

                def line(t, j, i):
                    d = j % DEPTH
                    pe.wait_ge(s_xb, t + 1)
                    wait(pe, s_o, t - DEPTH + 1)
                    pe.matmul(y_ps[:, d, :], ident[:, :], xb[:, d, :], start=True, stop=False)
                    pe.wait_ge(s_y, t + 1)
                    pe.matmul(y_ps[:, d, :], ident[:, :], y[:, d, :], start=False, stop=True).then_inc(s_yx, 1)
                tiles(pe, line, 1)

            @block.scalar
            def _(act):
                act.wait_ge(s_sum, TILES + 2)
                act.mul(mean[:, :], sum_ps[:, :], 1.0 / N_NODES).then_inc(s_mean, 1)

                def square(t, j, i):
                    act.wait_ge(s_d, t + 1)
                    wait(act, s_var, t - DEPTH + 1)
                    act.activation(sq[:, j % DEPTH, :], row(t), ACT.Square).then_inc(s_sq, 1)
                tiles(act, square, 1)
                act.wait_ge(s_var, TILES)
                act.activation(amp[:, :], var_ps[:, :], ACT.Sqrt, scale=1.0 / N_NODES,
                               bias=eps[:, 0:1]).then_inc(s_amp, 1)

                def norm(t, j, i):
                    a, b = (j - 2) % DEPTH, (j - 3) % DEPTH
                    if there(t - 2):
                        act.wait_ge(s_mv, t - 1)
                        wait(act, s_sh, t - 1 - DEPTH)
                        act.activation(std[:, a, :], mv[:, a, 1:2], ACT.Sqrt, bias=eps[:, 0:1]).then_inc(s_std, 1)
                    if there(t - 3):
                        act.wait_ge(s_sh, t - 2)
                        wait(act, s_out[b], 16 * (i * (SLOTS // DEPTH) + (j - 3) // DEPTH))
                        act.activation(o_sb[:, b, :], y_ps[:, b, :], ACT.Identity, scale=rstd[:, b, :],
                                       bias=shift[:, b, :]).then_inc(s_o, 1)
                        wait_apart(act, s_o, t - 2)
                        act.dma_start(out[bass.ds((t - 3) * P, P), :], o_sb[:, b, :]).then_inc(s_out[b], 16)
                tiles(act, norm, 1, 3)
                for d in range(DEPTH):
                    act.wait_ge(s_out[d], 16 * len(range(d, TILES, DEPTH)))

            @block.vector
            def _(dve):
                dve.memset(eps[:, :], 1e-5)
                dve.memset(sq[:, 0, :], 0.0)
                dve.scalar_tensor_tensor(out=rz[:, :, :], in0=agg[:, :, DIM + HEADS:AGG], scalar=1e-6,
                                         in1=agg[:, :, DIM:DIM + HEADS], op0=ALU.add,
                                         op1=ALU.add).then_inc(s_rz, 1)
                dve.wait_ge(s_rz, 1)
                dve.reciprocal(rz[:, :, :], rz[:, :, :]).then_inc(s_rz, 3)
                dve.wait_ge(s_rz, 4)

                def h_of(t, j, i):
                    if there(t):
                        h = row(t).rearrange("p (h d) -> p h d", d=D_HEAD)
                        r = rz[:, bass.ds(t, 1), :].rearrange("p a h -> p (a h)").unsqueeze(2).broadcast_to(
                            [P, HEADS, D_HEAD])
                        dve.tensor_tensor(h, h, r, ALU.mult).then_inc(s_h, 1)
                    if j % 2 and there(t - 1):
                        dve.wait_ge(s_h, t)
                        dve.wait_ge(s_ld[j - 1], 16 * (i + 1))
                        dve.tensor_tensor(row(t - 1), row(t - 1), x_sb[:, j - 1, :], ALU.add).then_inc(s_hd, 1)
                tiles(dve, h_of, 0, 1)
                dve.wait_ge(s_mean, 1)

                def centre(t, j, i):
                    dve.tensor_tensor(row(t), row(t), mean[:, :], ALU.subtract).then_inc(s_d, 1)
                tiles(dve, centre)
                dve.wait_ge(s_amp, 1)
                dve.reciprocal(amp[:, :], amp[:, :]).then_inc(s_amp, 1)
                dve.wait_ge(s_amp, 2)
                dve.wait_ge(s_par, 32)
                dve.tensor_tensor(amp[:, :], amp[:, :], gam[:, :], ALU.mult).then_inc(s_amp, 1)
                dve.wait_ge(s_amp, 3)

                def line(t, j, i):
                    a, b, c = j % DEPTH, (j - 2) % DEPTH, (j - 3) % DEPTH
                    if there(t):
                        wait(dve, s_yx, t - DEPTH + 1)
                        dve.tensor_tensor(y[:, a, :], row(t), amp[:, :], ALU.mult).then_inc(s_y, 1)
                    if there(t - 3):
                        dve.wait_ge(s_std, t - 2)
                        dve.reciprocal(rstd[:, c, :], std[:, c, :]).then_inc(s_rs, 1)
                    if there(t - 2):
                        dve.wait_ge(s_yx, t - 1)
                        dve.bn_stats(stats[:, b, :], y_ps[:, b, :]).then_inc(s_st, 1)
                    if there(t - 3):
                        dve.wait_ge(s_rs, t - 2)
                        dve.scalar_tensor_tensor(out=shift[:, c, :], in0=mv[:, c, 0:1], scalar=-1.0,
                                                 in1=rstd[:, c, :], op0=ALU.mult, op1=ALU.mult).then_inc(s_sh, 1)
                    if there(t - 2):
                        wait_apart(dve, s_st, t - 1)
                        dve.bn_aggr(mv[:, b, :], stats[:, b, :]).then_inc(s_mv, 1)
                tiles(dve, line, 1, 3)


def program(nc, xT, x, wq, wk, wv, gamma, beta, edges, dlast, out):
    kv_d = nc.dram_tensor("kv_d", (ROWS, 2 * DIM), F32, kind="Internal").ap()
    q_d = nc.dram_tensor("q_d", (ROWS, 2 * DIM), F32, kind="Internal").ap()
    t_d = nc.dram_tensor("t_d", (VCOLS,), I32, kind="Internal").ap()
    cnt_d = nc.dram_tensor("cnt_d", (64,), I32, kind="Internal").ap()
    with ExitStack() as ctx:
        def sb(name, shape, dt):
            return ctx.enter_context(nc.sbuf_tensor(name, shape, dt))

        tabs = (sb("src_t", [P, VCOLS], I32),
                sb("loc_t", [P, VCOLS], F32),
                sb("bits_row", [1, MASKS], I32),
                sb("cnt_row", [1, 64], I32),
                sb("iota_row", [P, P], F32),
                sb("ident", [P, P], F32))
        project(nc, xT, wq, wk, wv, edges, dlast, kv_d, q_d, t_d, cnt_d, tabs)
        agg = sb("agg", [P, TILES, AGG], F32)
        attend(nc, kv_d, q_d, tabs, agg)
        normalise(nc, x, gamma, beta, out, tabs[-1], agg)


def kernel(**inputs):
    import numpy as np
    import concourse.bacc as bacc
    from concourse.bass_utils import run_bass_kernel_spmd

    x = np.zeros((ROWS, DIM), np.float32)
    x[:N_NODES] = inputs["x"]
    edges = np.zeros((BLOCKS_IN * P, 2), np.int32)
    edges[:N_EDGES, 0] = inputs["src"]
    edges[:N_EDGES, 1] = inputs["dst"]
    edges[N_EDGES:BLOCKS * P, 1] = ROWS - 1
    edges[BLOCKS * P:, 1] = -1
    arrays = {
        "xT": np.ascontiguousarray(x.reshape(TILES, P, CHUNKS, P).transpose(0, 3, 2, 1)),
        "x": x,
        "wq": np.ascontiguousarray(inputs["L0_gnn_Wq"]),
        "wk": np.ascontiguousarray(inputs["L0_gnn_Wk"]),
        "wv": np.ascontiguousarray(inputs["L0_gnn_Wv"]),
        "gamma": np.ascontiguousarray(inputs["L0_gnn_bn_gamma"]).reshape(1, DIM),
        "beta": np.ascontiguousarray(inputs["L0_gnn_bn_beta"]).reshape(1, DIM),
        "edges": np.ascontiguousarray(edges.reshape(BLOCKS_IN, P, 2).transpose(0, 2, 1)).reshape(BLOCKS_IN, 2 * P),
        "dlast": np.ascontiguousarray(edges[P - 1::P, 1]).reshape(1, BLOCKS_IN),
    }
    nc = bacc.Bacc("TRN2", target_bir_lowering=False, num_devices=1)
    aps = {}
    for name, a in arrays.items():
        aps[name] = nc.dram_tensor(f"in_{name}", a.shape, mybir.dt.from_np(a.dtype), kind="ExternalInput").ap()
    out = nc.dram_tensor("out_rows", (ROWS, DIM), F32, kind="ExternalOutput").ap()
    program(nc, out=out, **aps)
    got = run_bass_kernel_spmd(nc, [{f"in_{n}": a for n, a in arrays.items()}], core_ids=[0])
    return got.results[0]["out_rows"][:N_NODES]
```
